# Optimizing a Trainium2 kernel written in Bass

```python
import numpy as np
import jax
import jax.numpy as jnp

def _softmax(x, axis=-1):
    return jax.nn.softmax(x, axis=axis)

def _gelu(x):
    return jax.nn.gelu(x, approximate=True)

def _silu(x):
    return jax.nn.silu(x)

def _sigmoid(x):
    return jax.nn.sigmoid(x)

def _layernorm(x, axis=-1, eps=1e-05):
    m = jnp.mean(x, axis=axis, keepdims=True)
    v = jnp.var(x, axis=axis, keepdims=True)
    return (x - m) / jnp.sqrt(v + eps)

def _scatter_add(tgt, idx, src, axis=0):
    return tgt.at[idx].add(src)

def _segment_sum(src, seg, n):
    return jax.ops.segment_sum(src, seg, n)
kernel_name = 'mk_xattn_ffn_d1_seqx_r4_182020'

def setup_inputs(seed: int=0):
    np.random.seed(seed)
    _w = jnp.asarray

    def _rec_inputs():
        import jax
        import jax.numpy as jnp
        _rk = jax.random.key(seed)
        x = 0.0003765 + 1 * jax.random.normal(jax.random.fold_in(_rk, 1), (16, 256, 512), jnp.float32)
        _lenS = 256 - jax.random.randint(jax.random.fold_in(_rk, 7), (16,), 0, max(1, 256 // 4) + 1, jnp.int32)
        _lenS2 = 256 - jax.random.randint(jax.random.fold_in(_rk, 8), (16,), 0, max(1, 256 // 4) + 1, jnp.int32)
        _ctx_2048P = jax.random.normal(jax.random.fold_in(_rk, 11), (16, 16, 512), jnp.float32)
        _ctx_2048c = jax.random.dirichlet(jax.random.fold_in(_rk, 511), 0.3 * jnp.ones((16,), jnp.float32), (16, 256))
        _ctx_2048t = jnp.einsum('bsk,bkd->bsd', _ctx_2048c, _ctx_2048P)
        _ctx_2048t = _ctx_2048t * jax.lax.rsqrt(jnp.mean(jnp.square(_ctx_2048t)) + 1e-12) * 0.953939
        ctx_2048 = -0.000292821 + 1.00034 * (_ctx_2048t + 0.3 * jax.random.normal(jax.random.fold_in(_rk, 611), (16, 256, 512), jnp.float32))
        return (x, ctx_2048)
    x, ctx_2048 = _rec_inputs()

    def _L0_xattn_setup():
        import jax, jax.numpy as jnp
        import numpy as np
        key = jax.random.key(seed)
        k1, k2, k3, k4, k5 = jax.random.split(key, 5)
        B, D_MODEL, L = (2, 256, 512)
        HEAD_DIM = 8
        H = D_MODEL // HEAD_DIM
        return {'k': jax.random.normal(k1, (B, D_MODEL, L), dtype=jnp.float32), 'v': jax.random.normal(k2, (B, D_MODEL, L), dtype=jnp.float32), 'q': jax.random.normal(k3, (B, D_MODEL, L), dtype=jnp.float32), 'ssm_kernel': jax.random.normal(k4, (H, L), dtype=jnp.float32), 'D': jax.random.normal(k5, (H,), dtype=jnp.float32), 'head_dim': HEAD_DIM}
    _L0_xattn_all = _L0_xattn_setup()
    _L0_xattn_in = {k: v for k, v in _L0_xattn_all.items() if k in ('ssm_kernel', 'D')}
    del _L0_xattn_all

    def _L0_ffn_setup():
        import jax, jax.numpy as jnp
        import numpy as np
        IN_F, OUT_F = (512, 512)
        N_EXPERTS, RANK, TOP_K = (8, 128, 2)
        key = jax.random.key(seed)
        k_x, k_r, k_a, k_b = jax.random.split(key, 4)
        hidden_states = jax.random.normal(k_x, (4, 1024, IN_F), dtype=jnp.float32)
        router_w = jax.random.normal(k_r, (IN_F, N_EXPERTS), dtype=jnp.float32) * IN_F ** (-0.5)
        Wa = jax.random.normal(k_a, (N_EXPERTS, IN_F, RANK), dtype=jnp.float32) * IN_F ** (-0.5)
        Wb = jax.random.normal(k_b, (N_EXPERTS, RANK, OUT_F), dtype=jnp.float32) * RANK ** (-0.5)
        return {'hidden_states': hidden_states, 'router_w': router_w, 'Wa': Wa, 'Wb': Wb}
    _L0_ffn_all = _L0_ffn_setup()
    _L0_ffn_in = {k: v for k, v in _L0_ffn_all.items() if k in ('router_w', 'Wa', 'Wb')}
    del _L0_ffn_all
    return {'x': x, 'ctx_2048': ctx_2048, 'L0_xattn_ssm_kernel': _L0_xattn_in['ssm_kernel'], 'L0_xattn_D': _L0_xattn_in['D'], 'L0_ffn_router_w': _L0_ffn_in['router_w'], 'L0_ffn_Wa': _L0_ffn_in['Wa'], 'L0_ffn_Wb': _L0_ffn_in['Wb']}

def reference(x, ctx_2048, L0_xattn_ssm_kernel, L0_xattn_D, L0_ffn_router_w, L0_ffn_Wa, L0_ffn_Wb):
    import jax
    import jax.numpy as jnp

    def _L0_xattn_ref(k, v, q, ssm_kernel, D, head_dim):
        import jax, jax.numpy as jnp
        import numpy as np
        B, HD, L = k.shape
        H = HD // head_dim
        fft_size = 2 * L
        k_ = k.reshape(B, H, head_dim, L)
        v_ = v.reshape(B, H, head_dim, L)
        q_ = q.reshape(B, H, head_dim, L)
        kv = jnp.einsum('bhil,bhjl->bijhl', k_, v_)
        kv_f = jnp.fft.rfft(kv, n=fft_size)
        kernel_f = jnp.fft.rfft(ssm_kernel, n=fft_size)
        y = jnp.fft.irfft(kv_f * kernel_f, n=fft_size)[..., :L]
        out = y + kv * D[None, None, None, :, None]
        out = jnp.einsum('bijhl,bhil->bjhl', out, q_)
        out = jnp.transpose(out, (0, 2, 1, 3)).reshape(B, H * head_dim, L)
        return out.astype(k.dtype)

    def _L0_ffn_ref(hidden_states, router_w, Wa, Wb):
        import jax, jax.numpy as jnp
        import numpy as np
        IN_F, OUT_F = (512, 512)
        N_EXPERTS, RANK, TOP_K = (8, 128, 2)
        B, S, D = hidden_states.shape
        x = hidden_states.reshape(-1, D)
        norm = jnp.maximum(jnp.linalg.norm(x, axis=-1, keepdims=True), 1e-12)
        router_logits = x / norm @ router_w
        routing_weights = jax.nn.softmax(router_logits.astype(jnp.float32), axis=-1)
        rw, selected_experts = jax.lax.top_k(routing_weights, TOP_K)
        rw = rw / jnp.sum(rw, axis=-1, keepdims=True)
        rw = rw.astype(hidden_states.dtype)
        combine = jnp.sum(jax.nn.one_hot(selected_experts, N_EXPERTS, dtype=rw.dtype) * rw[..., None], axis=1)
        out = jnp.zeros((x.shape[0], OUT_F), dtype=hidden_states.dtype)
        for e in range(N_EXPERTS):
            out = out + combine[:, e, None] * (x @ Wa[e] @ Wb[e])
        return out.reshape(B, S, OUT_F)
    x = x + _L0_xattn_ref(ctx_2048, ctx_2048, _layernorm(x, axis=-1), L0_xattn_ssm_kernel, L0_xattn_D, 8)
    x = x + _L0_ffn_ref(_layernorm(x, axis=-1), L0_ffn_router_w, L0_ffn_Wa, L0_ffn_Wb)
    return x

_drawn_inputs = setup_inputs


def setup_inputs(seed=0):
    import zlib

    import numpy as np

    out = dict(_drawn_inputs(seed))
    spreads = {}
    factors = {'L0_ffn_router_w': 5.157, 'L0_ffn_Wa': 4.433, 'L0_ffn_Wb': 4.433}
    for name, (base, spread) in spreads.items():
        noise = np.random.default_rng([zlib.crc32(name.encode()), seed]).standard_normal(out[name].shape)
        drawn = base * np.exp(spread * noise) if base else spread * noise
        out[name] = jnp.asarray(drawn.astype(out[name].dtype))
    for name, factor in factors.items():
        out[name] = (out[name] * factor).astype(out[name].dtype)
    return out
```

```python
from contextlib import ExitStack

import concourse.bass as bass
from concourse import mybir

F32 = mybir.dt.float32
F32R = mybir.dt.float32r
ALU = mybir.AluOpType
ACT = mybir.ActivationFunctionType
AX_X = mybir.AxisListType.X

P = 128
B = 16
HD = 8
H = 32
L = 512
NB = L // P
HALF = 2
BH = B // HALF
CH = HD * BH
REC = 36 * BH
D4 = 3 * CH
D0 = D4 + CH // 2
QREC = REC + 3 * BH
CREC = CH + 3 * BH
NREC = NB * HALF
G = 4
NG = H // G
T = G * P
E = 8
RANK = 128
EPS = 1e-5
HUGE = 3.0e38
USES = E + G
PAD = P + L

STEPS = [[], [("T", 0)], [("T", 1)], [("T", 2)],
         [("T", 3), ("L", 0)], [("R", 0)], [("S", 0)], [("S", 1), ("S", 2)],
         [("S", 3)], [("S", 4)], [("S", 5)], [("S", 6), ("S", 7)],
         [("O", 0)], [("O", 1)], [("O", 2)], [("O", 3)]]


def head(g, s):
    return g * G + s


def loads(g, s, ring):
    return g * (G // ring) + s // ring + 1


def before(g, s, n):
    return isinstance(g, int) and head(g, s) < n

SUMS = 10
ROUTE = 17


def build(nc, x_t, c_t, taps, skip, w_r, w_a, w_b, consts, select, out_t):
    padded = nc.dram_tensor("padded_taps", [H, PAD], F32, kind="Internal").ap()

    with ExitStack() as ctx:
        def sb(name, shape, dt=F32):
            return ctx.enter_context(nc.sbuf_tensor(name, shape, dt))

        def sem(name):
            return ctx.enter_context(nc.semaphore(name))

        def bank(name):
            return ctx.enter_context(nc.psum_tensor(name, [P, 512], F32))

        cst = sb("cst", [P, P + E])
        ident, preference = cst[:, 0:P], cst[:, P:P + E]
        sel_f = sb("sel_f", [40, E, P])
        sel = sb("sel", [40, E, P], F32R)
        minus_half = sb("minus_half", [P, G])
        wa = sb("wa", [P, NB, E, RANK])
        wb = sb("wb", [P, E, L])
        wr = sb("wr", [P, NB, E])
        kp = sb("kp", [H, PAD])
        skips = sb("skips", [H, 1])
        x_in = sb("x_in", [P, G, L])
        c_in = sb("c_in", [P, 2, NREC, CREC])
        toep = sb("toep", [P, 2, L])
        csum4 = sb("csum4", [P, NREC, CH // 2])
        csum2 = sb("csum2", [P, NREC, CH // 4])
        half = sb("half", [P, NREC, BH])
        csum1 = sb("csum1", [P, NREC, BH])
        csum = sb("csum", [P, NREC, BH])
        cdiff = sb("cdiff", [P, NREC, CH])
        pair = sb("pair", [P, 2, NREC, REC])
        qn = sb("qn", [P, L])
        qs = sb("qs", [P, 2, NREC, QREC])
        w = sb("w", [P, NREC, REC])
        u = sb("u", [P, NREC, CH])
        att = sb("att", [P, NREC, CH])
        stat1 = sb("stat1", [P, 6])
        mom1, mean1, dev1 = sb("mom1", [P, 2, 5]), sb("mean1", [P, 2]), sb("dev1", [P, 2])
        ve1 = sb("ve1", [P, 2])
        rstd1 = sb("rstd1", [P, 2])
        x2 = sb("x2", [P, G, L])
        stat2 = sb("stat2", [P, 6])
        mom2, mean2, dev2 = sb("mom2", [P, G, 5]), sb("mean2", [P, G]), sb("dev2", [P, G])
        ve2 = sb("ve2", [P, G])
        rstd2 = sb("rstd2", [P, G])
        nn = sb("nn", [P, G])
        nn2 = sb("nn2", [P, G])
        rlen = sb("rlen", [P, G])
        xn = sb("xn", [P, 2, L])
        xn_t = sb("xn_t", [P, NB, T])
        res = sb("res", [P, G, L])
        lg = sb("lg", [P, 6, G, E])
        red = sb("red", [P, 6, G])
        ex = sb("ex", [P, G, E])
        comb = sb("comb", [P, G, E])
        comb_t = sb("comb_t", [40, T], F32R)
        cw = sb("cw", [P, 2, T])
        hs = sb("hs", [P, E, T])

        y_ps = [[bank(f"y{i}{f}") for f in range(HALF)] for i in range(2)]
        t_ps = bank("t_ps")
        m_ps = bank("m_ps")
        e_ps = [bank("e0"), bank("e1")]

        s_const, s_w, s_taps = sem("const_loaded"), sem("weights_loaded"), sem("taps_loaded")
        s_pad0, s_padd, s_padw = sem("pad_zeroed"), sem("skip_added"), sem("padded_written")
        s_x = [sem(f"x_loaded{i}") for i in range(G)]
        s_c = [sem(f"c_loaded{i}") for i in range(2)]
        s_t = [sem(f"toep_loaded{i}") for i in range(2)]
        s_sel, s_selr, s_half = sem("comb_rows_zeroed"), sem("select_rounded"), sem("minus_half_ready")
        s_bn, s_mo1, s_ve1, s_rstd1 = sem("stats1"), sem("meanvar1"), sem("var_eps1"), sem("rstd1_ready")
        s_cs, s_csum, s_cd, s_pair = sem("channel_sum_steps"), sem("channel_sum"), sem("channel_diff"), sem("pairs_ready")
        s_qn, s_qT, s_qev, s_qs = sem("q_normed"), sem("q_transposed"), sem("q_evacuated"), sem("q_sums")
        s_y, s_wt = sem("conv_done"), sem("weighted")
        s_sum, s_att = sem("sum_steps"), sem("att_transposed")
        s_x2, s_bn2, s_mo2, s_ve2 = sem("x2_ready"), sem("stats2"), sem("meanvar2"), sem("var_eps2")
        s_rs2, s_nn0, s_nn, s_rl = sem("rstd2_ready"), sem("length_part"), sem("squared_length"), sem("rlength_ready")
        s_res, s_xn, s_xT, s_xev = sem("residual_kept"), sem("xn_ready"), sem("xn_transposed"), sem("xn_evacuated")
        s_lg, s_rt, s_ex = sem("logits"), sem("routing_steps"), sem("exp_done")
        s_cT, s_cH, s_cL = sem("combine_transposed"), sem("combine_high"), sem("combine_low")
        s_cb, s_cc = sem("combine_spread"), sem("combine_copied")
        s_e, s_eu = sem("expert_done"), sem("expert_used")
        s_out = [sem(f"stored{i}") for i in range(G)]

        block = ctx.enter_context(nc.Block())

        def run(eng, group):
            group(0, convs=True, experts=False, last=False)
            group(1, convs=True, experts=True, last=False)
            with eng.Fori(2, NG - 1) as g:
                group(g, convs=True, experts=True, last=False)
            group(NG - 1, convs=True, experts=True, last=True)
            group(NG, convs=False, experts=True, last=True)

        @block.sync
        def _(sp):
            def load_x(g, s):
                if not before(g, s, G):
                    sp.wait_ge(s_x2, head(g, s - G) + 1)
                sp.dma_start(x_in[:, s % G, :], x_t[head(g, s)]).then_inc(s_x[s % G], 16)

            def load_c(g, s):
                if not before(g, s, 2):
                    sp.wait_ge(s_pair, 2 * (head(g, s) - 1))
                sp.dma_start(c_in[:, s % 2], c_t[head(g, s)].rearrange("p (n c) -> p n c", n=NREC))\
                    .then_inc(s_c[s % 2], 16)

            def load_toeplitz(g, s):
                if not before(g, s, 2):
                    sp.wait_ge(s_y, NB * (head(g, s) - 1))
                sp.dma_start(toep[:, s % 2, :], bass.AP(padded.tensor, head(g, s) * PAD + 1, [[1, P], [1, L]]))\
                    .then_inc(s_t[s % 2], 16)

            load_x(0, 0)
            sp.dma_start(cst[:], consts).then_inc(s_const, 16)
            load_c(0, 0)
            sp.wait_ge(s_pad0, 1)
            sp.dma_start(kp[:, P:PAD], taps).then_inc(s_taps, 16)
            sp.dma_start(skips[:], skip).then_inc(s_taps, 16)
            load_x(0, 1)
            load_c(0, 1)
            sp.wait_ge(s_padd, 1)
            sp.dma_start(padded, kp[:]).then_inc(s_padw, 16)
            load_x(0, 2)
            sp.wait_ge(s_padw, 16)
            load_toeplitz(0, 0)
            sp.dma_start(sel_f[:], select).then_inc(s_w, 16)
            for n in range(NB):
                sp.dma_start(wa[:, n], w_a[:, n * P:(n + 1) * P, :].rearrange("e p n -> p e n")).then_inc(s_w, 16)
            sp.dma_start(wb[:], w_b.rearrange("e p n -> p e n")).then_inc(s_w, 16)
            sp.dma_start(wr[:], w_r.rearrange("(c p) e -> p c e", p=P)).then_inc(s_w, 16)

            def group(g, convs, experts, last):
                for s in range(G):
                    if convs and not (last and s + 1 >= G):
                        load_toeplitz(g, s + 1)
                    if convs and not (last and s + 2 >= G):
                        load_c(g, s + 2)
                    if convs and not (last and s + 3 >= G):
                        load_x(g, s + 3)
                if experts:
                    for i in range(G):
                        sp.wait_ge(s_eu, USES * (g - 1) + E + i + 1)
                        sp.dma_start(out_t[head(g - 1, i)], res[:, i, :]).then_inc(s_out[i], 16)

            run(sp, group)
            for i in range(G):
                sp.wait_ge(s_out[i], 16 * NG)

        @block.gpsimd
        def _(pool):
            def power(out, base, done):
                nc.gpsimd.tensor_tensor(out, base, minus_half[:, 0:1], ALU.pow).then_inc(done, 1)

            def prep(g, s):
                h = head(g, s)
                pool.wait_ge(s_c[s % 2], 16 * loads(g, s, 2))
                if not before(g, s, 1):
                    pool.wait_ge(s_cd, h)
                c = c_in[:, s % 2]
                nc.gpsimd.tensor_tensor(csum4[:], c[:, :, 0:32], c[:, :, 32:64], ALU.add).then_inc(s_cs, 1)
                pool.wait_ge(s_cs, 3 * h + 1)
                nc.gpsimd.tensor_tensor(csum2[:], csum4[:, :, 0:16], csum4[:, :, 16:32], ALU.add).then_inc(s_cs, 1)
                pool.wait_ge(s_cs, 3 * h + 2)
                nc.gpsimd.tensor_tensor(csum1[:], csum2[:, :, 0:8], csum2[:, :, 8:16], ALU.add).then_inc(s_cs, 1)
                pool.wait_ge(s_cs, 3 * h + 3)
                nc.gpsimd.tensor_tensor(csum[:], csum1[:], half[:], ALU.mult).then_inc(s_csum, 1)
                pool.wait_ge(s_ve1, 2 * h + 2)
                power(rstd1[:, s % 2:s % 2 + 1], ve1[:, s % 2:s % 2 + 1], s_rstd1)

            def q_sums(g, s):
                pool.wait_ge(s_qev, 2 * head(g, s) + 2)
                q = qs[:, s % 2]
                for d in (1, 2, 3):
                    nc.gpsimd.tensor_tensor(q[:, :, (d - 1) * CH:d * CH], q[:, :, D0:D0 + CH],
                                            q[:, :, D0 + d * BH:D0 + d * BH + CH], ALU.add).then_inc(s_qs, 1)
                nc.gpsimd.tensor_tensor(q[:, :, D4:D0], q[:, :, D0:D0 + 32], q[:, :, D0 + 32:D0 + 64], ALU.add)\
                    .then_inc(s_qs, 1)

            def lengths(g, s):
                h, i = head(g, s), s % G
                pool.wait_ge(s_ve2, 2 * h + 2)
                power(rstd2[:, i:i + 1], ve2[:, i:i + 1], s_rs2)
                pool.wait_ge(s_nn, h + 1)
                if s >= 0 and not before(g, 0, G):
                    pool.wait_ge(s_rt, ROUTE * (g - 1) + 1)
                power(rlen[:, i:i + 1], nn2[:, i:i + 1], s_rl)

            nc.gpsimd.memset(minus_half[:], -0.5).then_inc(s_half, 1)
            nc.gpsimd.memset(half[:], 0.5).then_inc(s_half, 1)
            nc.gpsimd.memset(comb_t[:].bitcast(F32), 0.0).then_inc(s_sel, 1)
            pool.wait_ge(s_half, 2)
            prep(0, 0)
            q_sums(0, 0)

            def group(g, convs, experts, last):
                for s in range(G):
                    if convs and not (last and s == G - 1):
                        prep(g, s + 1)
                    if (convs or s == 0) and not before(g, s, 1):
                        lengths(g, s - 1)
                    if convs and not (last and s == G - 1):
                        q_sums(g, s + 1)

            run(pool, group)

        @block.scalar
        def _(act):
            def q_out(g, s):
                h = head(g, s)
                act.wait_ge(s_qT, h + 1)
                if not before(g, s, 2):
                    act.wait_ge(s_wt, NB * (h - 1))
                src = t_ps[:].rearrange("p (n c) -> p n c", n=NREC)
                nc.scalar.copy(qs[:, s % 2, :, D0:D0 + CH], src).then_inc(s_qev, 1)
                nc.scalar.copy(qs[:, s % 2, :, REC:QREC], src[:, :, 0:3 * BH]).then_inc(s_qev, 1)

            def keep(g, i):
                act.wait_ge(s_x2, head(g - 1, i) + 1)
                if not before(g, 0, 2 * G):
                    act.wait_ge(s_out[i], 16 * (g - 1))
                nc.scalar.copy(res[:, i, :], x2[:, i, :]).then_inc(s_res, 1)

            def xn_out(g, i):
                act.wait_ge(s_xT, head(g - 1, i) + 1)
                nc.scalar.copy(xn_t[:, :, i * P:(i + 1) * P], m_ps[:].rearrange("p (c t) -> p c t", c=NB))\
                    .then_inc(s_xev, 1)

            def route(g):
                act.wait_ge(s_rt, ROUTE * (g - 1) + 3)
                nc.scalar.activation(ex[:], lg[:, 1], ACT.Exp).then_inc(s_ex, 1)
                act.wait_ge(s_cT, g)
                if before(g, 0, 2 * G):
                    act.wait_ge(s_sel, 1)
                nc.scalar.copy(comb_t[0:E, :], m_ps[0:E, :]).then_inc(s_cH, 1)

            def spread(g, e):
                act.wait_ge(s_cb, E * (g - 1) + e + 1)
                if e >= 2:
                    act.wait_ge(s_eu, USES * (g - 1) + e - 1)
                nc.scalar.copy(cw[:, e % 2, :], m_ps[:]).then_inc(s_cc, 1)

            def group(g, convs, experts, last):
                for s in range(G):
                    for r in range(NB):
                        if r == 2 and convs and not (last and s == G - 1):
                            q_out(g, s + 1)
                        for what, n in STEPS[s * NB + r] if experts else ():
                            if what == "T":
                                keep(g, n)
                                xn_out(g, n)
                            if what == "R":
                                route(g)
                            if what == "S":
                                spread(g, n)

            q_out(0, 0)
            run(act, group)

        @block.tensor
        def _(pe):
            def transpose_blocks(out, block_of, done):
                for n in range(NB):
                    turned = pe.matmul(out[:, n * P:(n + 1) * P], block_of(n), ident, start=(n == 0),
                                       stop=(n == NB - 1), is_transpose=True, skip_group_check=True)
                turned.then_inc(done, 1)

            def turn_q(g, s):
                h = head(g, s)
                pe.wait_ge(s_qn, h + 1)
                if not before(g, s, 2):
                    pe.wait_ge(s_x2, h - 1)
                transpose_blocks(t_ps, lambda n: qn[:, n * P:(n + 1) * P], s_qT)

            def convolve(g, s, r):
                h = head(g, s)
                if r == 0:
                    pe.wait_ge(s_t[s % 2], 16 * loads(g, s, 2))
                    pe.wait_ge(s_pair, 2 * (h + 1))
                if not (before(g, s, 1) and r < 2):
                    pe.wait_ge(s_wt, NB * h + r - 1)
                for f in range(HALF):
                    for n in range(r + 1):
                        product = pe.matmul(y_ps[r % 2][f][:, 0:REC], toep[:, s % 2, (r - n) * P:(r - n + 1) * P],
                                            pair[:, s % 2, n * HALF + f, :], start=(n == 0), stop=(n == r))
                product.then_inc(s_y, 1)

            def turn_attention(g, s):
                h = head(g, s)
                pe.wait_ge(s_sum, SUMS * (h + 1))
                pe.wait_ge(s_qev, 2 * min(h + 2, H) if isinstance(g, int) else 2 * (h + 2))
                transpose_blocks(t_ps, lambda n: att[:, n * HALF:(n + 1) * HALF, :], s_att)

            def turn_x(g, i):
                pe.wait_ge(s_xn, head(g - 1, i) + 1)
                if i > 0:
                    pe.wait_ge(s_xev, head(g - 1, i))
                elif not before(g, 0, 2 * G):
                    pe.wait_ge(s_cc, E * (g - 1))
                transpose_blocks(m_ps, lambda n: xn[:, i % 2, n * P:(n + 1) * P], s_xT)

            def logits(g):
                pe.wait_ge(s_xev, G * g)
                if before(g, 0, 2 * G):
                    pe.wait_ge(s_w, 16 * (NB + 3))
                for i in range(G):
                    for n in range(NB):
                        product = pe.matmul(m_ps[:, i * E:(i + 1) * E], xn_t[:, n, i * P:(i + 1) * P], wr[:, n, :],
                                            start=(i == 0 and n == 0), stop=(n == NB - 1), skip_group_check=True)
                product.then_inc(s_lg, 1)

            def turn_combine(g):
                pe.wait_ge(s_rt, ROUTE * g)
                for i in range(G):
                    turned = pe.matmul(m_ps[0:E, i * P:(i + 1) * P], comb[:, i, :], ident, start=(i == 0),
                                       stop=(i == G - 1), is_transpose=True, skip_group_check=True)
                turned.then_inc(s_cT, 1)

            def expert_bank(g, n):
                if n >= 2 or not before(g, 0, 2 * G):
                    pe.wait_ge(s_eu, USES * (g - 1) + n - 1)

            def hidden(g, e):
                if e == 0:
                    pe.wait_ge(s_cL, g)
                    if before(g, 0, 2 * G):
                        pe.wait_ge(s_selr, 1)
                else:
                    pe.wait_ge(s_cc, E * (g - 1) + e)
                pe.matmul(m_ps[:], sel[:, e, :], comb_t[:], start=True, stop=True).then_inc(s_cb, 1)
                expert_bank(g, e)
                for n in range(NB):
                    product = pe.matmul(e_ps[e % 2][:], wa[:, n, e, :], xn_t[:, n, :], start=(n == 0), stop=(n == NB - 1))
                product.then_inc(s_e, 1)

            def outputs(g, i):
                expert_bank(g, E + i)
                if i == 0:
                    pe.wait_ge(s_eu, USES * (g - 1) + E)
                for e in range(E):
                    product = pe.matmul(e_ps[i % 2][:], hs[:, e, i * P:(i + 1) * P], wb[:, e, :],
                                        start=(e == 0), stop=(e == E - 1))
                product.then_inc(s_e, 1)

            def group(g, convs, experts, last):
                for s in range(G):
                    for r in range(NB):
                        if convs:
                            convolve(g, s, r)
                        if r == 0 and (convs or s == 0) and not before(g, s, 1):
                            turn_attention(g, s - 1)
                        if r == 2 and convs and not (last and s == G - 1):
                            turn_q(g, s + 1)
                        for what, n in STEPS[s * NB + r] if experts else ():
                            if what == "T":
                                turn_x(g, n)
                            if what == "L":
                                logits(g)
                            if what == "R":
                                turn_combine(g)
                            if what == "S":
                                hidden(g, n)
                            if what == "O":
                                outputs(g, n)

            pe.wait_ge(s_const, 16)
            turn_q(0, 0)
            run(pe, group)

        @block.vector
        def _(dve):
            def variance(row, k, h, to, s_stats, s_steps, s_done):
                stat, mom, mean, dev, ve = to
                m = mom[:, k]
                nc.vector.bn_stats(stat[:], row).then_inc(s_stats, 1)
                dve.wait_ge(s_stats, h + 1)
                nc.vector.tensor_tensor(m[:, 0:3], stat[:, 0:3], stat[:, 3:6], ALU.add).then_inc(s_steps, 1)
                nc.vector.tensor_tensor(m[:, 3:4], stat[:, 1:2], stat[:, 4:5], ALU.subtract).then_inc(s_steps, 1)
                dve.wait_ge(s_steps, 3 * h + 2)
                nc.vector.tensor_scalar(mean[:, k:k + 1], m[:, 1:2], 0.5, None, ALU.mult)
                nc.vector.scalar_tensor_tensor(m[:, 4:5], m[:, 3:4], L / 4, m[:, 3:4], ALU.mult, ALU.mult).then_inc(s_steps, 1)
                dve.wait_ge(s_steps, 3 * h + 3)
                nc.vector.tensor_tensor(dev[:, k:k + 1], m[:, 4:5], m[:, 2:3], ALU.add).then_inc(s_done, 1)
                dve.wait_ge(s_done, 2 * h + 1)
                nc.vector.tensor_scalar(ve[:, k:k + 1], dev[:, k:k + 1], 1.0 / L, EPS, ALU.mult, ALU.add).then_inc(s_done, 1)

            def moments(g, s):
                h, k = head(g, s), s % 2
                dve.wait_ge(s_x[s % G], 16 * loads(g, s, G))
                variance(x_in[:, s % G, :], k, h, (stat1, mom1, mean1, dev1, ve1), s_bn, s_mo1, s_ve1)

            def norm_q(g, s):
                h, k = head(g, s), s % 2
                dve.wait_ge(s_rstd1, h + 1)
                if not before(g, s, 1):
                    dve.wait_ge(s_qT, h)
                nc.vector.tensor_scalar(qn[:], x_in[:, s % G, :], mean1[:, k:k + 1], rstd1[:, k:k + 1],
                                        ALU.subtract, ALU.mult).then_inc(s_qn, 1)

            def pairs(g, s):
                h, k = head(g, s), s % 2
                c = c_in[:, k]
                dve.wait_ge(s_csum, h + 1)
                if not before(g, s, 1):
                    dve.wait_ge(s_pair, 2 * h)
                nc.vector.tensor_tensor(
                    cdiff[:].rearrange("p n (k b) -> p n k b", b=BH), c[:, :, 0:CH].rearrange("p n (k b) -> p n k b", b=BH),
                    csum[:].unsqueeze(2).to_broadcast([P, NREC, HD, BH]), ALU.subtract).then_inc(s_cd, 1)
                if not before(g, s, 2):
                    dve.wait_ge(s_y, NB * (h - 1))
                for d in (1, 2, 3):
                    nc.vector.tensor_tensor(pair[:, k, :, (d - 1) * CH:d * CH], c[:, :, 0:CH],
                                            c[:, :, d * BH:d * BH + CH], ALU.mult)
                nc.vector.tensor_tensor(pair[:, k, :, D4:D0], c[:, :, 0:32], c[:, :, 32:64], ALU.mult).then_inc(s_pair, 1)
                dve.wait_ge(s_cd, h + 1)
                nc.vector.scalar_tensor_tensor(pair[:, k, :, D0:REC], cdiff[:], 2.0, c[:, :, 0:CH], ALU.mult, ALU.mult).then_inc(s_pair, 1)

            def weigh(g, s, r):
                h = head(g, s)
                dve.wait_ge(s_y, NB * h + r + 1)
                if r == 0:
                    dve.wait_ge(s_qs, NB * (h + 1))
                    if not before(g, s, 1):
                        dve.wait_ge(s_sum, SUMS * h)
                for f in range(HALF):
                    n = r * HALF + f
                    weighted = nc.vector.tensor_tensor(w[:, n, :], y_ps[r % 2][f][:, 0:REC], qs[:, s % 2, n, 0:REC], ALU.mult)
                weighted.then_inc(s_wt, 1)

            def sum_pairs(g, s):
                h = head(g, s)
                a = w[:, :, D0:REC]
                a2 = a.rearrange("p n (t c) -> p n t c", t=2)
                first = SUMS * h

                def add(out, in0, in1, after):
                    if after:
                        dve.wait_ge(s_sum, first + after)
                    nc.vector.tensor_tensor(out, in0, in1, ALU.add).then_inc(s_sum, 1)

                dve.wait_ge(s_wt, NB * (h + 1))
                add(a, a, w[:, :, 0:CH], 0)
                add(u[:], w[:, :, CH:2 * CH], w[:, :, 2 * CH:D4], 0)
                add(a2, a2, w[:, :, D4:D0].unsqueeze(2).to_broadcast([P, NREC, 2, CH // 2]), 1)
                add(a, a, u[:], 3)
                for d in (1, 2, 3):
                    k, lo, after = d * BH, (d - 1) * CH, 2 * d + 2
                    out = a
                    if d == 3:
                        out = att[:]
                        if not before(g, s, 1):
                            dve.wait_ge(s_att, h)
                    add(out[:, :, k:CH], a[:, :, k:CH], w[:, :, lo:lo + CH - k], after)
                    add(out[:, :, 0:k], a[:, :, 0:k], w[:, :, lo + CH - k:lo + CH], after)

            def residual(g, s):
                h, i = head(g, s), s % G
                dve.wait_ge(s_att, h + 1)
                if not before(g, s, G):
                    dve.wait_ge(s_res, h - G + 1)
                nc.vector.tensor_tensor(x2[:, i, :], t_ps[:], x_in[:, i, :], ALU.add).then_inc(s_x2, 1)
                dve.wait_ge(s_x2, h + 1)
                variance(x2[:, i, :], i, h, (stat2, mom2, mean2, dev2, ve2), s_bn2, s_mo2, s_ve2)
                dve.wait_ge(s_rs2, h + 1)
                nc.vector.scalar_tensor_tensor(nn[:, i:i + 1], rstd2[:, i:i + 1], rstd2[:, i:i + 1], dev2[:, i:i + 1],
                                               ALU.mult, ALU.mult).then_inc(s_nn0, 1)
                dve.wait_ge(s_nn0, h + 1)
                nc.vector.tensor_scalar(nn2[:, i:i + 1], nn[:, i:i + 1], 1e-24, None, ALU.max).then_inc(s_nn, 1)

            def norm_x(g, i):
                n = head(g - 1, i)
                dve.wait_ge(s_rs2, n + 1)
                if i >= 2 or not before(g, 0, 2 * G):
                    dve.wait_ge(s_xT, n - 1)
                nc.vector.tensor_scalar(xn[:, i % 2, :], x2[:, i, :], mean2[:, i:i + 1], rstd2[:, i:i + 1],
                                        ALU.subtract, ALU.mult).then_inc(s_xn, 1)

            def scale_logits(g):
                dve.wait_ge(s_lg, g)
                dve.wait_ge(s_rl, G * g)
                nc.vector.tensor_tensor(lg[:, 0], m_ps[:, 0:G * E].rearrange("p (i e) -> p i e", i=G),
                                        rlen[:].unsqueeze(2).to_broadcast([P, G, E]), ALU.mult).then_inc(s_rt, 1)

            def route(g):
                first = ROUTE * (g - 1)
                done = [1]
                wide = lambda a: a.unsqueeze(2).to_broadcast([P, G, E])
                lower = preference.unsqueeze(1).to_broadcast([P, G, E])

                def step(ins):
                    done[0] += 1
                    ins.then_inc(s_rt, 1)
                    dve.wait_ge(s_rt, first + done[0])

                dve.wait_ge(s_rt, first + 1)
                step(nc.vector.tensor_reduce(red[:, 0], lg[:, 0], AX_X, ALU.max))
                step(nc.vector.tensor_tensor(lg[:, 1], lg[:, 0], wide(red[:, 0]), ALU.subtract))
                step(nc.vector.scalar_tensor_tensor(lg[:, 2], lg[:, 1], 0.0, lower, ALU.is_ge, ALU.mult))
                step(nc.vector.tensor_reduce(red[:, 1], lg[:, 2], AX_X, ALU.max))
                step(nc.vector.tensor_tensor(lg[:, 3], lg[:, 2], wide(red[:, 1]), ALU.is_equal))
                step(nc.vector.scalar_tensor_tensor(lg[:, 4], lg[:, 3], -HUGE, lg[:, 1], ALU.mult, ALU.add))
                step(nc.vector.tensor_reduce(red[:, 2], lg[:, 4], AX_X, ALU.max))
                step(nc.vector.tensor_tensor(lg[:, 5], lg[:, 4], wide(red[:, 2]), ALU.is_equal))
                step(nc.vector.tensor_tensor(lg[:, 2], lg[:, 5], lower, ALU.mult))
                step(nc.vector.tensor_reduce(red[:, 3], lg[:, 2], AX_X, ALU.max))
                step(nc.vector.tensor_tensor(lg[:, 4], lg[:, 2], wide(red[:, 3]), ALU.is_equal))
                step(nc.vector.tensor_tensor(lg[:, 0], lg[:, 3], lg[:, 4], ALU.add))
                dve.wait_ge(s_ex, g)
                step(nc.vector.tensor_tensor(lg[:, 5], ex[:], lg[:, 0], ALU.mult))
                step(nc.vector.reduce_sum(red[:, 4], lg[:, 5], AX_X))
                step(nc.vector.reciprocal(red[:, 5], red[:, 4]))
                step(nc.vector.tensor_tensor(comb[:], lg[:, 5], wide(red[:, 5]), ALU.mult))
                dve.wait_ge(s_cH, g)
                nc.vector.tensor_tensor(comb_t[32:32 + E, :], m_ps[0:E, :], comb_t[0:E, :].bitcast(F32), ALU.subtract)\
                    .then_inc(s_cL, 1)

            def weigh_hidden(g, e):
                dve.wait_ge(s_e, USES * (g - 1) + e + 1)
                dve.wait_ge(s_cc, E * (g - 1) + e + 1)
                nc.vector.tensor_tensor(hs[:, e, :], e_ps[e % 2][:], cw[:, e % 2, :], ALU.mult).then_inc(s_eu, 1)

            def finish(g, i):
                dve.wait_ge(s_e, USES * (g - 1) + E + i + 1)
                dve.wait_ge(s_res, head(g - 1, i) + 1)
                nc.vector.tensor_tensor(res[:, i, :], e_ps[i % 2][:], res[:, i, :], ALU.add).then_inc(s_eu, 1)

            nc.vector.memset(kp[:, 0:P], 0.0).then_inc(s_pad0, 1)
            moments(0, 0)
            dve.wait_ge(s_taps, 32)
            nc.vector.tensor_tensor(kp[:, P:P + 1], kp[:, P:P + 1], skips[:], ALU.add).then_inc(s_padd, 1)
            norm_q(0, 0)
            pairs(0, 0)

            def group(g, convs, experts, last):
                for s in range(G):
                    more = convs and not (last and s == G - 1)
                    for r in range(NB):
                        if convs:
                            weigh(g, s, r)
                        if r == 0 and more:
                            moments(g, s + 1)
                        if r == 1 and (convs or s == 0) and not before(g, s, 1):
                            residual(g, s - 1)
                        if r == 1 and more:
                            norm_q(g, s + 1)
                        if r == 2 and more:
                            pairs(g, s + 1)
                        if r == NB - 1 and convs:
                            sum_pairs(g, s)
                        if experts and s == 0:
                            norm_x(g, r)
                        if before(g, 0, 1) and s == 1 and r == 0:
                            dve.wait_ge(s_w, 16 * (NB + 3))
                            nc.vector.tensor_copy(sel[:], sel_f[:]).then_inc(s_selr, 1)
                        for what, n in STEPS[s * NB + r] if experts else ():
                            if what == "L":
                                scale_logits(g)
                            if what == "R":
                                route(g)
                            if what == "S":
                                weigh_hidden(g, n)
                            if what == "O":
                                finish(g, n)

            run(dve, group)


def kernel(x, ctx_2048, L0_xattn_ssm_kernel, L0_xattn_D, L0_ffn_router_w, L0_ffn_Wa, L0_ffn_Wb):
    import numpy as np
    import concourse.bacc as bacc
    from concourse.bass_utils import run_bass_kernel_spmd

    x_t = np.asarray(x).reshape(HALF, BH, H, HD, L).transpose(2, 0, 3, 1, 4).reshape(H, P, L)
    c = np.asarray(ctx_2048).reshape(HALF, BH, H, HD, NB, P)[..., ::-1].transpose(2, 5, 4, 0, 3, 1)
    c_t = np.concatenate([c, c[:, :, :, :, 0:3]], axis=4).reshape(H, P, NREC * CREC)
    consts = np.concatenate([np.eye(P, dtype=np.float32),
                             np.tile(np.arange(E, 0, -1, dtype=np.float32), (P, 1))], axis=1)
    select = np.zeros((40, E, P), np.float32)
    for e in range(E):
        select[e, e] = select[32 + e, e] = 1.0

    ins = {"x_t": x_t, "c_t": c_t, "taps": np.asarray(L0_xattn_ssm_kernel), "skip": np.asarray(L0_xattn_D).reshape(H, 1),
           "w_r": np.asarray(L0_ffn_router_w), "w_a": np.asarray(L0_ffn_Wa), "w_b": np.asarray(L0_ffn_Wb),
           "consts": consts, "select": select}
    nc = bacc.Bacc("TRN2", target_bir_lowering=False, num_devices=1)
    arrays, args = {}, []
    for name, a in ins.items():
        a = np.ascontiguousarray(a)
        arrays[f"in_{name}_dram"] = a
        args.append(nc.dram_tensor(f"in_{name}_dram", a.shape, mybir.dt.from_np(a.dtype), kind="ExternalInput").ap())
    args.append(nc.dram_tensor("out_dram", [H, P, L], F32, kind="ExternalOutput").ap())
    build(nc, *args)
    r = run_bass_kernel_spmd(nc, [arrays], core_ids=[0])
    got = np.asarray(r.results[0]["out_dram"]).reshape(H, HALF, HD, BH, L)
    return np.ascontiguousarray(got.transpose(1, 3, 0, 2, 4).reshape(B, H * HD, L))
```

```python
from contextlib import ExitStack

import concourse.bass as bass
from concourse import mybir

F32 = mybir.dt.float32
F32R = mybir.dt.float32r
ALU = mybir.AluOpType
ACT = mybir.ActivationFunctionType
AX_X = mybir.AxisListType.X

P = 128
B = 16
HD = 8
H = 32
L = 512
NB = L // P
HALF = 2
BH = B // HALF
CH = HD * BH
REC = 36 * BH
D4 = 3 * CH
D0 = D4 + CH // 2
QREC = REC + 3 * BH
CREC = CH + 3 * BH
NREC = NB * HALF
G = 4
NG = H // G
HEADS = 2
E = 8
RANK = 128
EPS = 1e-5
HUGE = 3.0e38
PAD = P + L
PARTS = [(0, 0), (0, 1), (1, 0)]
TH = HEADS * P
USES = E + HEADS

FRONT = [[], [], [("T", 0)], [("T", 1)], [("L", 0)], [], [("R", 0)], []]
BACK = [[("S", 0), ("S", 1)], [("S", 2), ("S", 3)], [("S", 4), ("S", 5)], [("S", 6), ("S", 7)],
        [("O", (0, 0))], [("O", (0, 1))], [("O", (1, 0))], [("O", (1, 1))]]


def head(g, s):
    return g * G + s


def loads(g, s, ring):
    return g * (G // ring) + s // ring + 1


def before(g, s, n):
    return isinstance(g, int) and head(g, s) < n


def exists(g, s):
    return not isinstance(g, int) or 0 <= head(g, s) < H


def half_no(g, j):
    return HEADS * g + j


def half_exists(g, j):
    return not isinstance(g, int) or 0 <= half_no(g, j) < H // HEADS


def half_before(g, j, n):
    return isinstance(g, int) and half_no(g, j) < n


def tile(j, i):
    return (HEADS * j + i) % G


def expert_steps(g, s, r):
    j, p = s // HEADS, s % HEADS * NB + r
    back = [(what, j - 2, n) for what, n in BACK[p]] if half_exists(g, j - 2) else []
    front = [(what, j - 1, n) for what, n in FRONT[p]] if half_exists(g, j - 1) else []
    return back + front


SUMS = 10
ROUTE = 17


def build(nc, x_t, c_t, taps, skip, w_r, w_a, w_b, consts, select, out_t):
    padded = [nc.dram_tensor(f"padded_taps_{part}", [H, PAD], F32, kind="Internal").ap() for part in ("high", "low")]

    with ExitStack() as ctx:
        def sb(name, shape, dt=F32):
            return ctx.enter_context(nc.sbuf_tensor(name, shape, dt))

        def sem(name):
            return ctx.enter_context(nc.semaphore(name))

        def bank(name):
            return ctx.enter_context(nc.psum_tensor(name, [P, 512], F32))

        cst = sb("cst", [P, P + E])
        ident, preference = cst[:, 0:P], cst[:, P:P + E]
        sel = sb("sel", [40, E, P], F32R)
        minus_half = sb("minus_half", [P, G])
        wa = [sb(f"wa{k}", [P, NB, E, RANK], F32R) for k in range(2)]
        wb = sb("wb", [P, E, L])
        wr_f = sb("wr_f", [P, NB, E])
        wr = [sb(f"wr{k}", [P, NB, E], F32R) for k in range(2)]
        skips = sb("skips", [H, 1])
        x_in = sb("x_in", [P, G, L])
        c_in = sb("c_in", [P, 2, NREC, CREC])
        toep = [sb(f"toep{k}", [P, 2, L], F32R) for k in range(2)]
        csum4 = sb("csum4", [P, NREC, CH // 2])
        csum2 = sb("csum2", [P, NREC, CH // 4])
        half = sb("half", [P, NREC, BH])
        csum1 = sb("csum1", [P, NREC, BH])
        csum = sb("csum", [P, NREC, BH])
        cdiff = sb("cdiff", [P, NREC, CH])
        prod = sb("prod", [P, NREC, REC])
        pair = [sb(f"pair{k}", [P, 2, NREC, REC], F32R) for k in range(2)]
        kpp = [pair[k][0:H, 1].rearrange("p n c -> p (n c)")[:, 0:PAD] for k in range(2)]
        qn = sb("qn", [P, L])
        qs = sb("qs", [P, 2, NREC, QREC])
        w = sb("w", [P, NREC, REC])
        att = sb("att", [P, NREC, CH])
        kp = w[0:H].rearrange("p n c -> p (n c)")[:, 0:PAD]
        junk = sb("junk", [P, L])
        total1, nmean1, dev1 = sb("total1", [P, 2]), sb("nmean1", [P, 2]), sb("dev1", [P, 2])
        ve1 = sb("ve1", [P, 2])
        rstd1 = sb("rstd1", [P, 2])
        x2 = sb("x2", [P, G, L])
        total2, nmean2, dev2 = sb("total2", [P, G]), sb("nmean2", [P, G]), sb("dev2", [P, G])
        ve2 = sb("ve2", [P, G])
        rstd2 = sb("rstd2", [P, G])
        nn = sb("nn", [P, G])
        nn2 = sb("nn2", [P, G])
        rlen = sb("rlen", [P, G])
        xn = sb("xn", [P, 2, L])
        xn_t = [sb(f"xn_t{k}", [P, 2, NB, TH], F32R) for k in range(2)]
        res = sb("res", [P, G, L])
        lg = sb("lg", [P, 6, HEADS, E])
        red = sb("red", [P, 6, HEADS])
        ex = sb("ex", [P, HEADS, E])
        comb = sb("comb", [P, HEADS, E])
        comb_t = sb("comb_t", [40, TH], F32R)
        cw = sb("cw", [P, 2, TH])
        hs = sb("hs", [P, E, TH])
        wa_f = hs[:].rearrange("p e t -> p (e t)")
        sel_f = res[0:40].rearrange("p i l -> p (i l)")[:, 0:E * P]

        y_ps = [[bank(f"y{i}{f}") for f in range(HALF)] for i in range(2)]
        t_ps = bank("t_ps")
        m_ps = bank("m_ps")
        e_ps = [bank("e0"), bank("e1")]

        s_const, s_w, s_taps = sem("const_loaded"), sem("weights_loaded"), sem("taps_loaded")
        s_pad0, s_padd, s_padw = sem("pad_zeroed"), sem("padded_steps"), sem("padded_written")
        s_stage, s_wah, s_wal = sem("weights_staged"), sem("weights_high"), sem("weights_low")
        s_wrh, s_wrl = sem("router_high"), sem("router_low")
        s_wb = sem("output_weights_loaded")
        s_x = [sem(f"x_loaded{i}") for i in range(G)]
        s_c = [sem(f"c_loaded{i}") for i in range(2)]
        s_t = [sem(f"toep_loaded{i}") for i in range(2)]
        s_sel, s_selr, s_half = sem("comb_rows_zeroed"), sem("select_rounded"), sem("minus_half_ready")
        s_mo1, s_dev1, s_ve1, s_rstd1 = sem("mean_steps1"), sem("deviations1"), sem("var_eps1"), sem("rstd1_ready")
        s_cs, s_csum, s_cd, s_pair = sem("channel_sum_steps"), sem("channel_sum"), sem("channel_diff"), sem("pairs_ready")
        s_prod, s_ph = sem("products"), sem("pairs_high")
        s_qn, s_qT, s_qev, s_qs = sem("q_normed"), sem("q_transposed"), sem("q_evacuated"), sem("q_sums")
        s_y, s_wt = sem("conv_done"), sem("weighted")
        s_sum, s_att = sem("sum_steps"), sem("att_transposed")
        s_x2, s_mo2, s_dev2, s_ve2 = sem("x2_ready"), sem("mean_steps2"), sem("deviations2"), sem("var_eps2")
        s_rs2, s_nn0, s_nn, s_rl = sem("rstd2_ready"), sem("length_part"), sem("squared_length"), sem("rlength_ready")
        s_res, s_xn, s_xT, s_xev = sem("residual_kept"), sem("xn_ready"), sem("xn_transposed"), sem("xn_high")
        s_xlo = sem("xn_low")
        s_lg, s_rt, s_ex = sem("logits"), sem("routing_steps"), sem("exp_done")
        s_cT, s_cH, s_cL = sem("combine_transposed"), sem("combine_high"), sem("combine_low")
        s_cc = sem("combine_copied")
        s_e, s_eu = sem("expert_done"), sem("expert_used")
        s_out = [sem(f"stored{i}") for i in range(G)]

        block = ctx.enter_context(nc.Block())

        def run(eng, group):
            group(0)
            group(1)
            with eng.Fori(2, NG - 1) as g:
                group(g)
            group(NG - 1)
            group(NG)

        @block.sync
        def _(sp):
            def load_x(g, s):
                if not before(g, s, G):
                    sp.wait_ge(s_x2, head(g, s - G) + 1)
                sp.dma_start(x_in[:, s % G, :], x_t[head(g, s)]).then_inc(s_x[s % G], 16)

            def load_c(g, s):
                if not before(g, s, 2):
                    sp.wait_ge(s_prod, 2 * (head(g, s) - 1))
                sp.dma_start(c_in[:, s % 2], c_t[head(g, s)].rearrange("p (n c) -> p n c", n=NREC))\
                    .then_inc(s_c[s % 2], 16)

            def load_toeplitz(g, s):
                if not before(g, s, 2):
                    sp.wait_ge(s_y, NB * (head(g, s) - 1))
                for k in range(2):
                    sp.dma_start(toep[k][:, s % 2, :].bitcast(F32), bass.AP(padded[k].tensor, head(g, s) * PAD + 1, [[1, P], [1, L]]))\
                        .then_inc(s_t[s % 2], 16)

            load_x(0, 0)
            sp.dma_start(cst[:], consts).then_inc(s_const, 16)
            load_c(0, 0)
            sp.dma_start(kp[:, P:PAD], taps).then_inc(s_taps, 16)
            sp.dma_start(skips[:], skip).then_inc(s_taps, 16)
            load_x(0, 1)
            load_c(0, 1)
            sp.wait_ge(s_padd, 3)
            for k in range(2):
                sp.dma_start(padded[k], kpp[k].bitcast(F32)).then_inc(s_padw, 16)
            load_x(0, 2)
            sp.dma_start(sel_f, select).then_inc(s_w, 16)
            sp.dma_start(wr_f[:], w_r.rearrange("(c p) e -> p c e", p=P)).then_inc(s_w, 16)
            sp.wait_ge(s_padw, 32)
            load_toeplitz(0, 0)

            def stage(k):
                if k:
                    sp.wait_ge(s_wal, k)
                for n in range(2):
                    sp.dma_start(wa_f[:, n * E * RANK:(n + 1) * E * RANK].rearrange("p (e n) -> p e n", e=E),
                                 w_a[:, (2 * k + n) * P:(2 * k + n + 1) * P, :].rearrange("e p n -> p e n"))\
                        .then_inc(s_stage, 16)

            stage(0)
            sp.dma_start(wb[:], w_b.rearrange("e p n -> p e n")).then_inc(s_wb, 16)

            def group(g):
                for s in range(G):
                    j = s // HEADS
                    if exists(g, s + 1):
                        load_toeplitz(g, s + 1)
                    if exists(g, s + 2):
                        load_c(g, s + 2)
                    if s % HEADS == 0 and half_exists(g, j - 3):
                        store(g, j - 3, 1)
                    if exists(g, s + 3):
                        load_x(g, s + 3)
                    if before(g, s, 2) and s == 1:
                        stage(1)
                    if s % HEADS == 1 and half_exists(g, j - 2):
                        store(g, j - 2, 0)

            def store(g, j, i):
                k = tile(j, i)
                sp.wait_ge(s_eu, USES * half_no(g, j) + E + i + 1)
                sp.dma_start(out_t[head(g, HEADS * j + i)], res[:, k, :]).then_inc(s_out[k], 16)

            run(sp, group)
            store(NG, -1, 1)
            for i in range(G):
                sp.wait_ge(s_out[i], 16 * NG)

        @block.gpsimd
        def _(pool):
            def power(out, base, done):
                nc.gpsimd.tensor_tensor(out, base, minus_half[:, 0:1], ALU.pow).then_inc(done, 1)

            def prep(g, s):
                h = head(g, s)
                pool.wait_ge(s_c[s % 2], 16 * loads(g, s, 2))
                if not before(g, s, 1):
                    pool.wait_ge(s_cd, h)
                c = c_in[:, s % 2]
                nc.gpsimd.tensor_tensor(csum4[:], c[:, :, 0:32], c[:, :, 32:64], ALU.add).then_inc(s_cs, 1)
                pool.wait_ge(s_cs, 3 * h + 1)
                nc.gpsimd.tensor_tensor(csum2[:], csum4[:, :, 0:16], csum4[:, :, 16:32], ALU.add).then_inc(s_cs, 1)
                pool.wait_ge(s_cs, 3 * h + 2)
                nc.gpsimd.tensor_tensor(csum1[:], csum2[:, :, 0:8], csum2[:, :, 8:16], ALU.add).then_inc(s_cs, 1)
                pool.wait_ge(s_cs, 3 * h + 3)
                nc.gpsimd.tensor_tensor(csum[:], csum1[:], half[:], ALU.mult).then_inc(s_csum, 1)
                pool.wait_ge(s_ve1, h + 1)
                power(rstd1[:, s % 2:s % 2 + 1], ve1[:, s % 2:s % 2 + 1], s_rstd1)

            def q_sums(g, s):
                pool.wait_ge(s_qev, 2 * head(g, s) + 2)
                q = qs[:, s % 2]
                for d in (1, 2, 3):
                    nc.gpsimd.tensor_tensor(q[:, :, (d - 1) * CH:d * CH], q[:, :, D0:D0 + CH],
                                            q[:, :, D0 + d * BH:D0 + d * BH + CH], ALU.add).then_inc(s_qs, 1)
                nc.gpsimd.tensor_tensor(q[:, :, D4:D0], q[:, :, D0:D0 + 32], q[:, :, D0 + 32:D0 + 64], ALU.add)\
                    .then_inc(s_qs, 1)

            def lengths(g, s):
                h, i = head(g, s), s % G
                pool.wait_ge(s_ve2, h + 1)
                power(rstd2[:, i:i + 1], ve2[:, i:i + 1], s_rs2)
                pool.wait_ge(s_nn, h + 1)
                j = s // HEADS
                if not half_before(g, j, 2):
                    pool.wait_ge(s_rt, ROUTE * (half_no(g, j) - 2) + 1)
                power(rlen[:, i:i + 1], nn2[:, i:i + 1], s_rl)

            nc.gpsimd.memset(minus_half[:], -0.5).then_inc(s_half, 1)
            nc.gpsimd.memset(half[:], 0.5).then_inc(s_half, 1)
            nc.gpsimd.memset(comb_t[:].bitcast(F32), 0.0).then_inc(s_sel, 1)
            pool.wait_ge(s_half, 2)
            prep(0, 0)
            q_sums(0, 0)

            def group(g):
                for s in range(G):
                    if exists(g, s + 1):
                        prep(g, s + 1)
                    if exists(g, s - 1):
                        lengths(g, s - 1)
                    if exists(g, s + 1):
                        q_sums(g, s + 1)

            run(pool, group)

        @block.scalar
        def _(act):
            def q_out(g, s):
                h = head(g, s)
                act.wait_ge(s_qT, h + 1)
                if not before(g, s, 2):
                    act.wait_ge(s_wt, NB * (h - 1))
                src = t_ps[:].rearrange("p (n c) -> p n c", n=NREC)
                nc.scalar.copy(qs[:, s % 2, :, D0:D0 + CH], src).then_inc(s_qev, 1)
                nc.scalar.copy(qs[:, s % 2, :, REC:QREC], src[:, :, 0:3 * BH]).then_inc(s_qev, 1)

            def moments(row, h, k, total, nmean, dev, steps, done):
                nc.scalar.activation(junk[:], row, ACT.Copy, accum_out=total[:, k:k + 1]).then_inc(steps, 1)
                act.wait_ge(steps, 2 * h + 1)
                nc.scalar.mul(nmean[:, k:k + 1], total[:, k:k + 1], -1.0 / L).then_inc(steps, 1)
                act.wait_ge(steps, 2 * h + 2)
                nc.scalar.activation(junk[:], row, ACT.Square, bias=nmean[:, k:k + 1], accum_out=dev[:, k:k + 1])\
                    .then_inc(done, 1)

            def moments1(g, s):
                h, k = head(g, s), s % 2
                act.wait_ge(s_x[s % G], 16 * loads(g, s, G))
                if not before(g, s, 2):
                    act.wait_ge(s_qn, h - 1)
                if not before(g, s, 3):
                    act.wait_ge(s_dev2, h - 2)
                elif h:
                    act.wait_ge(s_dev1, h)
                moments(x_in[:, s % G, :], h, k, total1, nmean1, dev1, s_mo1, s_dev1)

            def moments2(g, s):
                h, i = head(g, s), s % G
                act.wait_ge(s_x2, h + 1)
                act.wait_ge(s_dev1, min(h + 3, H) if isinstance(g, int) else h + 3)
                moments(x2[:, i, :], h, i, total2, nmean2, dev2, s_mo2, s_dev2)

            def split_pairs(g, s):
                h, k = head(g, s), s % 2
                act.wait_ge(s_prod, 2 * (h + 1))
                if not before(g, s, 2):
                    act.wait_ge(s_y, NB * (h - 1))
                elif s == 1:
                    act.wait_ge(s_padw, 32)
                nc.scalar.copy(pair[0][:, k], prod[:]).then_inc(s_ph, 1)

            def keep(g, j, i):
                k, n = tile(j, i), head(g, HEADS * j + i)
                act.wait_ge(s_x2, n + 1)
                if half_before(g, j, 2):
                    act.wait_ge(s_selr, 1)
                else:
                    act.wait_ge(s_out[k], 16 * (g + j // 2))
                nc.scalar.copy(res[:, k, :], x2[:, k, :]).then_inc(s_res, 1)

            def xn_out(g, j, i):
                act.wait_ge(s_xT, half_no(g, j) * HEADS + i + 1)
                if not half_before(g, j, 2):
                    act.wait_ge(s_e, USES * (half_no(g, j) - 2) + E)
                nc.scalar.copy(xn_t[0][:, j % 2, :, i * P:(i + 1) * P], m_ps[:].rearrange("p (c t) -> p c t", c=NB))\
                    .then_inc(s_xev, 1)

            def exponentials(g, j):
                act.wait_ge(s_rt, ROUTE * half_no(g, j) + 3)
                nc.scalar.activation(ex[:], lg[:, 1], ACT.Exp).then_inc(s_ex, 1)

            def combine_high(g, j):
                act.wait_ge(s_cT, half_no(g, j) + 1)
                if half_before(g, j, 1):
                    act.wait_ge(s_sel, 1)
                else:
                    act.wait_ge(s_e, USES * (half_no(g, j) - 1) + E)
                nc.scalar.copy(comb_t[0:E, :], m_ps[0:E, 0:TH]).then_inc(s_cH, 1)

            def copy_weights(g, j, e):
                u = half_no(g, j)
                act.wait_ge(s_e, USES * u + e + 1)
                if e >= 2:
                    act.wait_ge(s_eu, USES * u + e - 1)
                nc.scalar.copy(cw[:, e % 2, :], e_ps[e % 2][:, TH:2 * TH]).then_inc(s_cc, 1)

            def front(step, g, s, *n):
                if half_exists(g, s // HEADS - 1):
                    step(g, s // HEADS - 1, *n)

            def back(step, g, s, *n):
                if half_exists(g, s // HEADS - 2):
                    step(g, s // HEADS - 2, *n)

            def even_head(g, s):
                if exists(g, s + 1):
                    moments1(g, s + 1)
                back(copy_weights, g, s, 0)
                back(copy_weights, g, s, 1)
                front(keep, g, s, 0)
                if exists(g, s - 1):
                    moments2(g, s - 1)
                back(copy_weights, g, s, 2)
                back(copy_weights, g, s, 3)
                if exists(g, s + 1):
                    q_out(g, s + 1)
                back(copy_weights, g, s, 4)
                if exists(g, s + 1):
                    split_pairs(g, s + 1)
                back(copy_weights, g, s, 5)
                front(xn_out, g, s, 0)
                back(copy_weights, g, s, 6)
                back(copy_weights, g, s, 7)
                front(xn_out, g, s, 1)

            def odd_head(g, s):
                if exists(g, s + 1):
                    moments1(g, s + 1)
                if exists(g, s - 1):
                    moments2(g, s - 1)
                front(keep, g, s, 1)
                front(exponentials, g, s)
                if exists(g, s + 1):
                    split_pairs(g, s + 1)
                    q_out(g, s + 1)
                front(combine_high, g, s)

            def group(g):
                for s in range(G):
                    (odd_head if s % HEADS else even_head)(g, s)
                    if before(g, s, 2):
                        act.wait_ge(s_stage, 32 * (s + 1))
                        nc.scalar.copy(wa[0][:, 2 * s:2 * s + 2].rearrange("p n e r -> p (n e r)"), wa_f).then_inc(s_wah, 1)
                    if before(g, s, 2) and s == 1:
                        act.wait_ge(s_w, 32)
                        nc.scalar.copy(sel[:].rearrange("p e m -> p (e m)"), sel_f).then_inc(s_selr, 1)
                        nc.scalar.copy(wr[0][:], wr_f[:]).then_inc(s_wrh, 1)

            moments1(0, 0)
            split_pairs(0, 0)
            q_out(0, 0)
            run(act, group)

        @block.tensor
        def _(pe):
            def transpose_blocks(out, block_of, done):
                for n in range(NB):
                    turned = pe.matmul(out[:, n * P:(n + 1) * P], block_of(n), ident, start=(n == 0),
                                       stop=(n == NB - 1), is_transpose=True, skip_group_check=True)
                turned.then_inc(done, 1)

            def turn_q(g, s):
                h = head(g, s)
                pe.wait_ge(s_qn, h + 1)
                if not before(g, s, 2):
                    pe.wait_ge(s_x2, h - 1)
                transpose_blocks(t_ps, lambda n: qn[:, n * P:(n + 1) * P], s_qT)

            def convolve(g, s, r):
                h = head(g, s)
                if r == 0:
                    pe.wait_ge(s_t[s % 2], 32 * loads(g, s, 2))
                    pe.wait_ge(s_pair, h + 1)
                if not (before(g, s, 1) and r < 2):
                    pe.wait_ge(s_wt, NB * h + r - 1)
                for f in range(HALF):
                    for n in range(r + 1):
                        for a, b in PARTS:
                            product = pe.matmul(y_ps[r % 2][f][:, 0:REC], toep[a][:, s % 2, (r - n) * P:(r - n + 1) * P],
                                                pair[b][:, s % 2, n * HALF + f, :], start=(n == 0 and (a, b) == PARTS[0]),
                                                stop=(n == r and (a, b) == PARTS[-1]))
                product.then_inc(s_y, 1)

            def turn_attention(g, s):
                h = head(g, s)
                pe.wait_ge(s_sum, SUMS * (h + 1))
                pe.wait_ge(s_qev, 2 * min(h + 2, H) if isinstance(g, int) else 2 * (h + 2))
                transpose_blocks(t_ps, lambda n: att[:, n * HALF:(n + 1) * HALF, :], s_att)

            def turn_x(g, j, i):
                n = half_no(g, j) * HEADS + i
                pe.wait_ge(s_xn, n + 1)
                if i > 0:
                    pe.wait_ge(s_xlo, n)
                elif not half_before(g, j, 1):
                    pe.wait_ge(s_cL, half_no(g, j))
                transpose_blocks(m_ps, lambda b: xn[:, i, b * P:(b + 1) * P], s_xT)

            def logits(g, j):
                pe.wait_ge(s_xlo, HEADS * (half_no(g, j) + 1))
                if half_before(g, j, 1):
                    pe.wait_ge(s_wrl, 1)
                for i in range(HEADS):
                    for n in range(NB):
                        for a, b in PARTS:
                            product = pe.matmul(m_ps[:, i * E:(i + 1) * E], xn_t[a][:, j % 2, n, i * P:(i + 1) * P],
                                                wr[b][:, n, :], start=(i == 0 and n == 0 and (a, b) == PARTS[0]),
                                                stop=(i == HEADS - 1 and n == NB - 1 and (a, b) == PARTS[-1]),
                                                skip_group_check=True)
                product.then_inc(s_lg, 1)

            def turn_combine(u):
                pe.wait_ge(s_rt, ROUTE * (u + 1))
                for i in range(HEADS):
                    turned = pe.matmul(m_ps[0:E, i * P:(i + 1) * P], comb[:, i, :], ident, start=(i == 0),
                                       stop=(i == HEADS - 1), is_transpose=True, skip_group_check=True)
                turned.then_inc(s_cT, 1)

            def expert_bank(g, j, use):
                if use >= 2 or not half_before(g, j, 1):
                    pe.wait_ge(s_eu, USES * half_no(g, j) + use - 1)

            def hidden(g, j, e):
                if e == 0:
                    pe.wait_ge(s_cL, half_no(g, j) + 1)
                    if half_before(g, j, 1):
                        pe.wait_ge(s_selr, 1)
                        pe.wait_ge(s_wal, 2)
                expert_bank(g, j, e)
                pe.matmul(e_ps[e % 2][:, TH:2 * TH], sel[:, e, :], comb_t[:], start=True, stop=False, skip_group_check=True)
                for c in range(NB):
                    for a, b in PARTS:
                        product = pe.matmul(e_ps[e % 2][:, 0:TH], wa[a][:, c, e, :], xn_t[b][:, j % 2, c, :], start=False,
                                            stop=(c == NB - 1 and (a, b) == PARTS[-1]), skip_group_check=True)
                product.then_inc(s_e, 1)

            def outputs(g, j, i, part):
                if part == 0:
                    expert_bank(g, j, E + i)
                    if half_before(g, j, 1) and i == 0:
                        pe.wait_ge(s_wb, 16)
                elif i == 0:
                    pe.wait_ge(s_eu, USES * half_no(g, j) + E)
                for e in range(part * E // 2, (part + 1) * E // 2):
                    product = pe.matmul(e_ps[i][:], hs[:, e, i * P:(i + 1) * P], wb[:, e, :],
                                        start=(e == 0), stop=(e == E - 1))
                if part == 1:
                    product.then_inc(s_e, 1)

            def experts(g, s, r):
                for what, j, n in expert_steps(g, s, r):
                    if what == "T":
                        turn_x(g, j, n)
                    if what == "L":
                        logits(g, j)
                    if what == "R":
                        turn_combine(half_no(g, j))
                    if what == "S":
                        hidden(g, j, n)
                    if what == "O":
                        outputs(g, j, *n)

            def group(g):
                for s in range(G):
                    for r in range(NB):
                        if exists(g, s):
                            convolve(g, s, r)
                        if r == 1 and exists(g, s - 1):
                            turn_attention(g, s - 1)
                        if r == 2 and exists(g, s + 1):
                            turn_q(g, s + 1)
                        experts(g, s, r)

            pe.wait_ge(s_const, 16)
            turn_q(0, 0)
            run(pe, group)

        @block.vector
        def _(dve):
            def var_eps(h, k, dev, ve, s_dev, s_ve):
                dve.wait_ge(s_dev, h + 1)
                nc.vector.tensor_scalar(ve[:, k:k + 1], dev[:, k:k + 1], 1.0 / L, EPS, ALU.mult, ALU.add).then_inc(s_ve, 1)

            def norm_q(g, s):
                h, k = head(g, s), s % 2
                dve.wait_ge(s_rstd1, h + 1)
                if not before(g, s, 1):
                    dve.wait_ge(s_qT, h)
                nc.vector.tensor_scalar(qn[:], x_in[:, s % G, :], nmean1[:, k:k + 1], rstd1[:, k:k + 1],
                                        ALU.add, ALU.mult).then_inc(s_qn, 1)

            def products_by_one(g, s):
                h = head(g, s)
                c = c_in[:, s % 2]
                dve.wait_ge(s_csum, h + 1)
                if not before(g, s, 1):
                    dve.wait_ge(s_pair, h)
                nc.vector.tensor_tensor(
                    cdiff[:].rearrange("p n (k b) -> p n k b", b=BH), c[:, :, 0:CH].rearrange("p n (k b) -> p n k b", b=BH),
                    csum[:].unsqueeze(2).to_broadcast([P, NREC, HD, BH]), ALU.subtract).then_inc(s_cd, 1)
                product(c, 1)

            def product(c, d):
                return nc.vector.tensor_tensor(prod[:, :, (d - 1) * CH:d * CH], c[:, :, 0:CH],
                                               c[:, :, d * BH:d * BH + CH], ALU.mult)

            def products(g, s):
                h = head(g, s)
                c = c_in[:, s % 2]
                product(c, 2)
                product(c, 3)
                nc.vector.tensor_tensor(prod[:, :, D4:D0], c[:, :, 0:32], c[:, :, 32:64], ALU.mult).then_inc(s_prod, 1)
                dve.wait_ge(s_cd, h + 1)
                nc.vector.scalar_tensor_tensor(prod[:, :, D0:REC], cdiff[:], 2.0, c[:, :, 0:CH], ALU.mult, ALU.mult)\
                    .then_inc(s_prod, 1)

            def split_pairs(g, s):
                h, k = head(g, s), s % 2
                dve.wait_ge(s_ph, h + 1)
                nc.vector.tensor_tensor(pair[1][:, k], prod[:], pair[0][:, k].bitcast(F32), ALU.subtract).then_inc(s_pair, 1)

            def weigh(g, s, r):
                h = head(g, s)
                dve.wait_ge(s_y, NB * h + r + 1)
                if r == 0:
                    dve.wait_ge(s_qs, NB * (h + 1))
                    if not before(g, s, 1):
                        dve.wait_ge(s_sum, SUMS * h)
                for f in range(HALF):
                    n = r * HALF + f
                    weighted = nc.vector.tensor_tensor(w[:, n, :], y_ps[r % 2][f][:, 0:REC], qs[:, s % 2, n, 0:REC], ALU.mult)
                weighted.then_inc(s_wt, 1)

            def sum_pairs(g, s, part):
                h = head(g, s)
                a = w[:, :, D0:REC]
                a2 = a.rearrange("p n (t c) -> p n t c", t=2)
                first = SUMS * h

                def add(out, in0, in1, after):
                    if after:
                        dve.wait_ge(s_sum, first + after)
                    nc.vector.tensor_tensor(out, in0, in1, ALU.add).then_inc(s_sum, 1)

                if part == 0:
                    dve.wait_ge(s_wt, NB * (h + 1))
                    add(a, a, w[:, :, 0:CH], 0)
                    if not before(g, s, 1):
                        dve.wait_ge(s_att, h)
                    add(att[:], w[:, :, CH:2 * CH], w[:, :, 2 * CH:D4], 0)
                if part == 1:
                    add(a2, a2, w[:, :, D4:D0].unsqueeze(2).to_broadcast([P, NREC, 2, CH // 2]), 1)
                    add(a, a, att[:], 3)
                for d in {0: (), 1: (1,), 2: (2, 3)}[part]:
                    k, lo, after = d * BH, (d - 1) * CH, 2 * d + 2
                    out = att[:] if d == 3 else a
                    add(out[:, :, k:CH], a[:, :, k:CH], w[:, :, lo:lo + CH - k], after)
                    add(out[:, :, 0:k], a[:, :, 0:k], w[:, :, lo + CH - k:lo + CH], after)

            def residual(g, s):
                h, i = head(g, s), s % G
                dve.wait_ge(s_att, h + 1)
                if not before(g, s, G):
                    dve.wait_ge(s_res, h - G + 1)
                nc.vector.tensor_tensor(x2[:, i, :], t_ps[:], x_in[:, i, :], ALU.add).then_inc(s_x2, 1)
                dve.wait_ge(s_x2, h + 1)

            def lengths(g, s):
                h, i = head(g, s), s % G
                var_eps(h, i, dev2, ve2, s_dev2, s_ve2)
                dve.wait_ge(s_rs2, h + 1)
                nc.vector.scalar_tensor_tensor(nn[:, i:i + 1], rstd2[:, i:i + 1], rstd2[:, i:i + 1], dev2[:, i:i + 1],
                                               ALU.mult, ALU.mult).then_inc(s_nn0, 1)
                dve.wait_ge(s_nn0, h + 1)
                nc.vector.tensor_scalar(nn2[:, i:i + 1], nn[:, i:i + 1], 1e-24, None, ALU.max).then_inc(s_nn, 1)

            def norm_x(g, j, i):
                k, n = tile(j, i), head(g, HEADS * j + i)
                dve.wait_ge(s_rs2, n + 1)
                if not half_before(g, j, 1):
                    dve.wait_ge(s_xT, n - 1)
                nc.vector.tensor_scalar(xn[:, i, :], x2[:, k, :], nmean2[:, k:k + 1], rstd2[:, k:k + 1],
                                        ALU.add, ALU.mult).then_inc(s_xn, 1)

            def xn_low(g, j, i):
                dve.wait_ge(s_xev, HEADS * half_no(g, j) + i + 1)
                cols = slice(i * P, (i + 1) * P)
                nc.vector.tensor_tensor(xn_t[1][:, j % 2, :, cols], m_ps[:].rearrange("p (c t) -> p c t", c=NB),
                                        xn_t[0][:, j % 2, :, cols].bitcast(F32), ALU.subtract).then_inc(s_xlo, 1)

            def scale_logits(g, j):
                u, k = half_no(g, j), tile(j, 0)
                dve.wait_ge(s_lg, u + 1)
                dve.wait_ge(s_rl, HEADS * (u + 1))
                nc.vector.tensor_tensor(lg[:, 0], m_ps[:, 0:HEADS * E].rearrange("p (i e) -> p i e", i=HEADS),
                                        rlen[:, k:k + HEADS].unsqueeze(2).to_broadcast([P, HEADS, E]), ALU.mult)\
                    .then_inc(s_rt, 1)

            def route(g, j):
                scale_logits(g, j)
                u = half_no(g, j)
                first = ROUTE * u
                done = [1]
                wide = lambda a: a.unsqueeze(2).to_broadcast([P, HEADS, E])
                lower = preference.unsqueeze(1).to_broadcast([P, HEADS, E])

                def step(ins):
                    done[0] += 1
                    ins.then_inc(s_rt, 1)
                    dve.wait_ge(s_rt, first + done[0])

                dve.wait_ge(s_rt, first + 1)
                step(nc.vector.tensor_reduce(red[:, 0], lg[:, 0], AX_X, ALU.max))
                step(nc.vector.tensor_tensor(lg[:, 1], lg[:, 0], wide(red[:, 0]), ALU.subtract))
                step(nc.vector.scalar_tensor_tensor(lg[:, 2], lg[:, 1], 0.0, lower, ALU.is_ge, ALU.mult))
                step(nc.vector.tensor_reduce(red[:, 1], lg[:, 2], AX_X, ALU.max))
                step(nc.vector.tensor_tensor(lg[:, 3], lg[:, 2], wide(red[:, 1]), ALU.is_equal))
                step(nc.vector.scalar_tensor_tensor(lg[:, 4], lg[:, 3], -HUGE, lg[:, 1], ALU.mult, ALU.add))
                step(nc.vector.tensor_reduce(red[:, 2], lg[:, 4], AX_X, ALU.max))
                step(nc.vector.tensor_tensor(lg[:, 5], lg[:, 4], wide(red[:, 2]), ALU.is_equal))
                step(nc.vector.tensor_tensor(lg[:, 2], lg[:, 5], lower, ALU.mult))
                step(nc.vector.tensor_reduce(red[:, 3], lg[:, 2], AX_X, ALU.max))
                step(nc.vector.tensor_tensor(lg[:, 4], lg[:, 2], wide(red[:, 3]), ALU.is_equal))
                step(nc.vector.tensor_tensor(lg[:, 0], lg[:, 3], lg[:, 4], ALU.add))
                dve.wait_ge(s_ex, u + 1)
                step(nc.vector.tensor_tensor(lg[:, 5], ex[:], lg[:, 0], ALU.mult))
                step(nc.vector.reduce_sum(red[:, 4], lg[:, 5], AX_X))
                step(nc.vector.reciprocal(red[:, 5], red[:, 4]))
                step(nc.vector.tensor_tensor(comb[:], lg[:, 5], wide(red[:, 5]), ALU.mult))

            def combine_low(g, j):
                u = half_no(g, j)
                dve.wait_ge(s_cH, u + 1)
                nc.vector.tensor_tensor(comb_t[32:32 + E, :], m_ps[0:E, 0:TH], comb_t[0:E, :].bitcast(F32), ALU.subtract)\
                    .then_inc(s_cL, 1)

            def weigh_hidden(g, j, e):
                dve.wait_ge(s_cc, E * half_no(g, j) + e + 1)
                nc.vector.tensor_tensor(hs[:, e, :], e_ps[e % 2][:, 0:TH], cw[:, e % 2, :], ALU.mult)\
                    .then_inc(s_eu, 1)

            def finish(g, j, i):
                k = tile(j, i)
                dve.wait_ge(s_e, USES * half_no(g, j) + E + i + 1)
                dve.wait_ge(s_res, head(g, HEADS * j + i) + 1)
                nc.vector.tensor_tensor(res[:, k, :], e_ps[i][:], res[:, k, :], ALU.add).then_inc(s_eu, 1)

            nc.vector.memset(kp[:, 0:P], 0.0)
            dve.wait_ge(s_taps, 32)
            nc.vector.tensor_tensor(kp[:, P:P + 1], kp[:, P:P + 1], skips[:], ALU.add).then_inc(s_padd, 1)
            dve.wait_ge(s_padd, 1)
            nc.vector.tensor_copy(kpp[0], kp).then_inc(s_padd, 1)
            dve.wait_ge(s_padd, 2)
            nc.vector.tensor_tensor(kpp[1], kp, kpp[0].bitcast(F32), ALU.subtract).then_inc(s_padd, 1)
            var_eps(0, 0, dev1, ve1, s_dev1, s_ve1)
            norm_q(0, 0)
            products_by_one(0, 0)
            products(0, 0)
            split_pairs(0, 0)

            def front(step, g, s, *n):
                if half_exists(g, s // HEADS - 1):
                    step(g, s // HEADS - 1, *n)

            def back(step, g, s, *n):
                if half_exists(g, s // HEADS - 2):
                    step(g, s // HEADS - 2, *n)

            def even_head(g, s):
                this, following, preceding = exists(g, s), exists(g, s + 1), exists(g, s - 1)
                if following:
                    var_eps(head(g, s + 1), (s + 1) % 2, dev1, ve1, s_dev1, s_ve1)
                if preceding:
                    sum_pairs(g, s - 1, 2)
                if this:
                    weigh(g, s, 0)
                back(weigh_hidden, g, s, 0)
                back(weigh_hidden, g, s, 1)
                if following:
                    norm_q(g, s + 1)
                if preceding:
                    residual(g, s - 1)
                if following:
                    products_by_one(g, s + 1)
                back(weigh_hidden, g, s, 2)
                if this:
                    weigh(g, s, 1)
                back(weigh_hidden, g, s, 3)
                if following:
                    products(g, s + 1)
                if preceding:
                    lengths(g, s - 1)
                front(norm_x, g, s, 0)
                if this:
                    weigh(g, s, 2)
                back(weigh_hidden, g, s, 4)
                front(norm_x, g, s, 1)
                if following:
                    split_pairs(g, s + 1)
                back(weigh_hidden, g, s, 5)
                front(xn_low, g, s, 0)
                if this:
                    weigh(g, s, 3)
                    sum_pairs(g, s, 0)
                back(weigh_hidden, g, s, 6)
                if this:
                    sum_pairs(g, s, 1)
                back(weigh_hidden, g, s, 7)
                front(xn_low, g, s, 1)

            def odd_head(g, s):
                this, following, preceding = exists(g, s), exists(g, s + 1), exists(g, s - 1)
                if following:
                    var_eps(head(g, s + 1), (s + 1) % 2, dev1, ve1, s_dev1, s_ve1)
                if preceding:
                    sum_pairs(g, s - 1, 2)
                if this:
                    weigh(g, s, 0)
                if following:
                    norm_q(g, s + 1)
                    products_by_one(g, s + 1)
                if preceding:
                    residual(g, s - 1)
                if this:
                    weigh(g, s, 1)
                if following:
                    products(g, s + 1)
                if preceding:
                    lengths(g, s - 1)
                front(route, g, s)
                if this:
                    weigh(g, s, 2)
                back(finish, g, s, 0)
                if following:
                    split_pairs(g, s + 1)
                front(combine_low, g, s)
                if this:
                    weigh(g, s, 3)
                    sum_pairs(g, s, 0)
                    sum_pairs(g, s, 1)
                back(finish, g, s, 1)

            def group(g):
                for s in range(G):
                    (odd_head if s % HEADS else even_head)(g, s)
                    if before(g, s, 3) and s in (1, 2):
                        dve.wait_ge(s_wah, s)
                        part = slice(2 * s - 2, 2 * s)
                        nc.vector.tensor_tensor(wa[1][:, part].rearrange("p n e r -> p (n e r)"), wa_f,
                                                wa[0][:, part].rearrange("p n e r -> p (n e r)").bitcast(F32),
                                                ALU.subtract).then_inc(s_wal, 1)
                    if before(g, s, 2) and s == 1:
                        dve.wait_ge(s_wrh, 1)
                        nc.vector.tensor_tensor(wr[1][:], wr_f[:], wr[0][:].bitcast(F32), ALU.subtract).then_inc(s_wrl, 1)

            run(dve, group)


def kernel(x, ctx_2048, L0_xattn_ssm_kernel, L0_xattn_D, L0_ffn_router_w, L0_ffn_Wa, L0_ffn_Wb):
    import numpy as np
    import concourse.bacc as bacc
    from concourse.bass_utils import run_bass_kernel_spmd

    x_t = np.asarray(x).reshape(HALF, BH, H, HD, L).transpose(2, 0, 3, 1, 4).reshape(H, P, L)
    c = np.asarray(ctx_2048).reshape(HALF, BH, H, HD, NB, P)[..., ::-1].transpose(2, 5, 4, 0, 3, 1)
    c_t = np.concatenate([c, c[:, :, :, :, 0:3]], axis=4).reshape(H, P, NREC * CREC)
    consts = np.concatenate([np.eye(P, dtype=np.float32),
                             np.tile(np.arange(E, 0, -1, dtype=np.float32), (P, 1))], axis=1)
    select = np.zeros((40, E, P), np.float32)
    for e in range(E):
        select[e, e] = select[32 + e, e] = 1.0

    ins = {"x_t": x_t, "c_t": c_t, "taps": np.asarray(L0_xattn_ssm_kernel), "skip": np.asarray(L0_xattn_D).reshape(H, 1),
           "w_r": np.asarray(L0_ffn_router_w), "w_a": np.asarray(L0_ffn_Wa), "w_b": np.asarray(L0_ffn_Wb),
           "consts": consts, "select": select}
    nc = bacc.Bacc("TRN2", target_bir_lowering=False, num_devices=1)
    arrays, args = {}, []
    for name, a in ins.items():
        a = np.ascontiguousarray(a)
        arrays[f"in_{name}_dram"] = a
        args.append(nc.dram_tensor(f"in_{name}_dram", a.shape, mybir.dt.from_np(a.dtype), kind="ExternalInput").ap())
    args.append(nc.dram_tensor("out_dram", [H, P, L], F32, kind="ExternalOutput").ap())
    build(nc, *args)
    r = run_bass_kernel_spmd(nc, [arrays], core_ids=[0])
    got = np.asarray(r.results[0]["out_dram"]).reshape(H, HALF, HD, BH, L)
    return np.ascontiguousarray(got.transpose(1, 3, 0, 2, 4).reshape(B, H * HD, L))
```

```python
from contextlib import ExitStack

import concourse.bass as bass
from concourse import mybir

F32 = mybir.dt.float32
F32R = mybir.dt.float32r
ALU = mybir.AluOpType
ACT = mybir.ActivationFunctionType
AX_X = mybir.AxisListType.X

P = 128
B = 16
HD = 8
H = 32
L = 512
NB = L // P
HALF = 2
BH = B // HALF
CH = HD * BH
REC = 36 * BH
D4 = 3 * CH
D0 = D4 + CH // 2
QREC = REC + 3 * BH
CREC = CH + 3 * BH
NREC = NB * HALF
G = 4
NG = H // G
HEADS = 2
E = 8
RANK = 128
EPS = 1e-5
HUGE = 3.0e38
PAD = P + L
PARTS = [(0, 0), (0, 1), (1, 0)]
ROWS = HEADS * P
USES = E + HEADS

FRONT = [[], [], [("T", 0)], [("T", 1)], [], [("L", 0)], [("R", 0)], []]
BACK = [[("S", 0), ("S", 1)], [("S", 2), ("S", 3)], [("S", 4), ("S", 5)], [("S", 6), ("S", 7)],
        [("O", (0, 0))], [("O", (0, 1))], [("O", (1, 0))], [("O", (1, 1))]]


def head(g, s):
    return g * G + s


def loads(g, s, ring):
    return g * (G // ring) + s // ring + 1


def before(g, s, n):
    return isinstance(g, int) and head(g, s) < n


def exists(g, s):
    return not isinstance(g, int) or 0 <= head(g, s) < H


def duo_no(g, j):
    return HEADS * g + j


def duo_exists(g, j):
    return not isinstance(g, int) or 0 <= duo_no(g, j) < H // HEADS


def duo_before(g, j, n):
    return isinstance(g, int) and duo_no(g, j) < n


def tile(j, i):
    return (HEADS * j + i) % G


def expert_steps(g, s, r):
    j, p = s // HEADS, s % HEADS * NB + r
    back = [(what, j - 2, n) for what, n in BACK[p]] if duo_exists(g, j - 2) else []
    front = [(what, j - 1, n) for what, n in FRONT[p]] if duo_exists(g, j - 1) else []
    return back + front


SUMS = 9
ROUTE = 19


def build(nc, x_t, c_t, taps, skip, w_r, w_a, w_b, consts, out_t):
    padded = [nc.dram_tensor(f"padded_taps_{part}", [H, PAD], F32, kind="Internal").ap() for part in ("high", "low")]
    combine = nc.dram_tensor("combine_weights", [E, ROWS], F32, kind="Internal").ap()

    with ExitStack() as ctx:
        def sb(name, shape, dt=F32):
            return ctx.enter_context(nc.sbuf_tensor(name, shape, dt))

        def parts(name, shape):
            high = sb(name + "_high", shape, F32R)
            place = nc.sbuf_base
            low = sb(name + "_low", shape, F32R)
            return (high, low), nc.alloc_sbuf_tensor_at(name, shape, F32, offset=place)

        def sem(name):
            return ctx.enter_context(nc.semaphore(name))

        def bank(name):
            return ctx.enter_context(nc.psum_tensor(name, [P, 512], F32))

        cst = sb("cst", [P, P + E])
        ident, preference = cst[:, 0:P], cst[:, P:P + E]
        minus_half = sb("minus_half", [P, G])
        wa, wa_f = parts("wa", [P, NB, E, RANK])
        wb, wb_f = parts("wb", [P, E, L])
        wr, wr_f = sb("wr", [P, NB, 2, E], F32R), sb("wr_f", [P, NB, E])
        skips = sb("skips", [H, 1])
        x_in = sb("x_in", [P, G, L])
        c_in = sb("c_in", [P, 2, NREC, CREC])
        toep = [sb(f"toep{k}", [P, 2, L], F32R) for k in range(2)]
        half = sb("half", [P, NREC, BH])
        csum = sb("csum", [P, NREC, BH])
        pair, prod = parts("pair", [P, 2, NREC, REC])
        kpp = [pair[k][0:H, 1].rearrange("p n c -> p (n c)")[:, 0:PAD] for k in range(2)]
        qn = sb("qn", [P, L])
        qs = sb("qs", [P, 2, NREC, QREC])
        w = sb("w", [P, NREC, REC])
        att = sb("att", [P, NREC, CH])
        kp = w[0:H].rearrange("p n c -> p (n c)")[:, 0:PAD]
        total1, nmean1, dev1 = sb("total1", [P, 2]), sb("nmean1", [P, 2]), sb("dev1", [P, 2])
        ve1 = sb("ve1", [P, 2])
        rstd1, shift1 = sb("rstd1", [P, 2]), sb("shift1", [P, 2])
        total2, nmean2, dev2 = sb("total2", [P, G]), sb("nmean2", [P, G]), sb("dev2", [P, G])
        ve2 = sb("ve2", [P, G])
        rstd2, shift2 = sb("rstd2", [P, G]), sb("shift2", [P, G])
        nn = sb("nn", [P, G])
        nn2 = sb("nn2", [P, G])
        rlen = sb("rlen", [P, G])
        xn = sb("xn", [P, L])
        junk = xn
        xn_t = [sb(f"xn_t{k}", [P, 2, NB, ROWS], F32R) for k in range(2)]
        res = sb("res", [P, G, L])
        lg = sb("lg", [P, 6, HEADS, E])
        red = sb("red", [P, 6, HEADS])
        ex = sb("ex", [P, HEADS, E])
        comb = sb("comb", [P, HEADS, E])
        comb_t = sb("comb_t", [E, ROWS])
        cw = sb("cw", [P, E, ROWS])
        hs, hw = parts("hidden", [P, E, ROWS])

        y_ps = [[bank(f"y{i}{f}") for f in range(HALF)] for i in range(2)]
        t_ps = bank("t_ps")
        m_ps = bank("m_ps")
        e_ps = [bank("e0"), bank("e1")]

        s_const, s_taps = sem("const_loaded"), sem("taps_loaded")
        s_padd, s_padw = sem("padded_steps"), sem("padded_written")
        s_high, s_low = sem("weights_high"), sem("weights_low")
        s_load = [sem(f"weights_loaded{k}") for k in range(NB + 5)]
        s_x = [sem(f"x_loaded{i}") for i in range(G)]
        s_c = [sem(f"c_loaded{i}") for i in range(2)]
        s_t = [sem(f"toep_loaded{i}") for i in range(2)]
        s_half = sem("halves_ready")
        s_mo1, s_dev1, s_ve1, s_rstd1 = sem("mean_steps1"), sem("deviations1"), sem("var_eps1"), sem("rstd1_ready")
        s_cs, s_csum, s_cd, s_pair = sem("channel_sum_steps"), sem("channel_sum"), sem("channel_diff"), sem("pairs_ready")
        s_prod, s_ph = sem("products"), sem("pairs_high")
        s_sh1, s_sh2 = sem("shift1_ready"), sem("shift2_ready")
        s_d23 = sem("part_sums")
        s_qn, s_qT, s_qev, s_qs = sem("q_normed"), sem("q_transposed"), sem("q_evacuated"), sem("q_sums")
        s_y, s_wt = sem("conv_done"), sem("weighted")
        s_sum, s_att = sem("sum_steps"), sem("att_transposed")
        s_x2, s_mo2, s_dev2, s_ve2 = sem("x2_ready"), sem("mean_steps2"), sem("deviations2"), sem("var_eps2")
        s_rs2, s_nn0, s_nn, s_rl = sem("rstd2_ready"), sem("length_part"), sem("squared_length"), sem("rlength_ready")
        s_res, s_xn, s_xT, s_xev = sem("residual_kept"), sem("xn_ready"), sem("xn_transposed"), sem("xn_high")
        s_xlo = sem("xn_low")
        s_lg, s_rt, s_ex = sem("logits"), sem("routing_steps"), sem("exp_done")
        s_cT, s_cS, s_cD = sem("combine_transposed"), sem("combine_in_sbuf"), sem("combine_written")
        s_cw = [sem(f"combine_spread{k}") for k in range(2)]
        s_hh, s_hl = sem("hidden_high"), sem("hidden_low")
        s_e, s_eu = sem("expert_done"), sem("expert_used")
        s_out = [sem(f"stored{i}") for i in range(G)]

        weights = [(wr[:, :, 0], wr[:, :, 1], wr_f[:])] + [[k[:, c] for k in (*wa, wa_f)] for c in range(NB)]
        weights += [[k[:, n:n + 2] for k in (*wb, wb_f)] for n in range(0, E, 2)]
        split_beside = [(0, 1, 2), (3, 4), (5, 6), (7, 8)]

        block = ctx.enter_context(nc.Block())

        def run(eng, group):
            group(0)
            group(1)
            with eng.Fori(2, NG - 1) as g:
                group(g)
            group(NG - 1)
            group(NG)

        @block.sync
        def _(sp):
            def load_x(g, s):
                if not before(g, s, G):
                    sp.wait_ge(s_res, head(g, s) - G + 1)
                    sp.wait_ge(s_xn, head(g, s) - G + 1)
                sp.dma_start(x_in[:, s % G, :], x_t[head(g, s)]).then_inc(s_x[s % G], 16)

            def load_c(g, s):
                if not before(g, s, 2):
                    sp.wait_ge(s_prod, head(g, s) - 1)
                sp.dma_start(c_in[:, s % 2], c_t[head(g, s)].rearrange("p (n c) -> p n c", n=NREC))\
                    .then_inc(s_c[s % 2], 16)

            def load_toeplitz(g, s):
                if not before(g, s, 2):
                    sp.wait_ge(s_y, NB * (head(g, s) - 1))
                for k in range(2):
                    sp.dma_start(toep[k][:, s % 2, :].bitcast(F32),
                                 bass.AP(padded[k].tensor, head(g, s) * PAD + 1, [[1, P], [1, L]])).then_inc(s_t[s % 2], 16)

            sp.dma_start(kp[:, P:PAD], taps).then_inc(s_taps, 16)
            sp.dma_start(skips[:], skip).then_inc(s_taps, 16)
            load_c(0, 0)
            load_x(0, 0)
            sp.dma_start(cst[:], consts).then_inc(s_const, 16)
            load_x(0, 1)
            load_c(0, 1)
            sp.wait_ge(s_padd, 3)
            for k in range(2):
                sp.dma_start(padded[k], kpp[k].bitcast(F32)).then_inc(s_padw, 16)
            sp.dma_start(wr_f[:], w_r.rearrange("(c p) e -> p c e", p=P)).then_inc(s_load[0], 16)
            sp.wait_ge(s_padw, 32)
            load_toeplitz(0, 0)

            for c in range(NB):
                sp.dma_start(wa_f[:, c], w_a[:, c * P:(c + 1) * P, :].rearrange("e p n -> p e n"))\
                    .then_inc(s_load[1 + c], 16)
            for n in range(E // 2):
                part = slice(2 * n, 2 * n + 2)
                sp.dma_start(wb_f[:, part], w_b[part].rearrange("e p n -> p e n"))\
                    .then_inc(s_load[1 + NB + n], 16)

            def group(g):
                for s in range(G):
                    j = s // HEADS
                    if exists(g, s + 1):
                        load_toeplitz(g, s + 1)
                    if exists(g, s + 2):
                        load_c(g, s + 2)
                    if s % HEADS == 0 and duo_exists(g, j - 3):
                        store(g, j - 3, 1)
                    if exists(g, s + 2):
                        load_x(g, s + 2)
                    if s % HEADS == 1 and duo_exists(g, j - 2):
                        store(g, j - 2, 0)
                    if s % HEADS == 1 and duo_exists(g, j - 1):
                        spread_combine(g, j - 1)

            def spread_combine(g, j):
                u = duo_no(g, j)
                sp.wait_ge(s_cS, u + 1)
                sp.dma_start(combine, comb_t[:]).then_inc(s_cD, 16)
                sp.wait_ge(s_cD, 16 * (u + 1))
                for k in range(2):
                    part = slice(k * E // 2, (k + 1) * E // 2)
                    sp.dma_start(cw[:, part].rearrange("p e t -> p (e t)"),
                                 bass.AP(combine.tensor, k * E // 2 * ROWS, [[0, P], [1, E // 2 * ROWS]])).then_inc(s_cw[k], 16)

            def store(g, j, i):
                k = tile(j, i)
                sp.wait_ge(s_eu, USES * duo_no(g, j) + E + i + 1)
                sp.dma_start(out_t[head(g, HEADS * j + i)], res[:, k, :]).then_inc(s_out[k], 16)

            run(sp, group)
            store(NG, -1, 1)
            for i in range(G):
                sp.wait_ge(s_out[i], 16 * NG)

        @block.gpsimd
        def _(pool):
            def power(out, base, done):
                nc.gpsimd.tensor_tensor(out, base, minus_half[:, 0:1], ALU.pow).then_inc(done, 1)

            def shift(out, nmean, rstd, done):
                nc.gpsimd.tensor_tensor(out, nmean, rstd, ALU.mult).then_inc(done, 1)

            def prep(g, s):
                h, k = head(g, s), s % 2
                pool.wait_ge(s_c[k], 16 * loads(g, s, 2))
                if not before(g, s, 1):
                    pool.wait_ge(s_cd, h)
                if not before(g, s, 2):
                    pool.wait_ge(s_y, NB * (h - 1))
                elif s == 1:
                    pool.wait_ge(s_padw, 32)
                c = c_in[:, k]
                sum2, sum4, sum8 = (prod[:, k, :, D0 + lo:D0 + hi] for lo, hi in ((0, 32), (32, 48), (48, 56)))
                nc.gpsimd.tensor_tensor(sum2, c[:, :, 0:32], c[:, :, 32:64], ALU.add).then_inc(s_cs, 1)
                pool.wait_ge(s_cs, 3 * h + 1)
                nc.gpsimd.tensor_tensor(sum4, sum2[:, :, 0:16], sum2[:, :, 16:32], ALU.add).then_inc(s_cs, 1)
                pool.wait_ge(s_cs, 3 * h + 2)
                nc.gpsimd.tensor_tensor(sum8, sum4[:, :, 0:8], sum4[:, :, 8:16], ALU.add).then_inc(s_cs, 1)
                pool.wait_ge(s_cs, 3 * h + 3)
                nc.gpsimd.tensor_tensor(csum[:], sum8, half[:], ALU.mult).then_inc(s_csum, 1)
                pool.wait_ge(s_csum, h + 1)
                nc.gpsimd.tensor_tensor(
                    prod[:, k, :, D0:REC].rearrange("p n (k b) -> p n k b", b=BH),
                    c[:, :, 0:CH].rearrange("p n (k b) -> p n k b", b=BH),
                    csum[:].unsqueeze(2).to_broadcast([P, NREC, HD, BH]), ALU.subtract).then_inc(s_cd, 1)
                pool.wait_ge(s_ve1, h + 1)
                power(rstd1[:, k:k + 1], ve1[:, k:k + 1], s_rstd1)
                pool.wait_ge(s_rstd1, h + 1)
                shift(shift1[:, k:k + 1], nmean1[:, k:k + 1], rstd1[:, k:k + 1], s_sh1)

            def q_sums(g, s):
                pool.wait_ge(s_qev, 2 * head(g, s) + 2)
                q = qs[:, s % 2]
                for d in (1, 2, 3):
                    nc.gpsimd.tensor_tensor(q[:, :, (d - 1) * CH:d * CH], q[:, :, D0:D0 + CH],
                                            q[:, :, D0 + d * BH:D0 + d * BH + CH], ALU.add).then_inc(s_qs, 1)
                nc.gpsimd.tensor_tensor(q[:, :, D4:D0], q[:, :, D0:D0 + 32], q[:, :, D0 + 32:D0 + 64], ALU.add)\
                    .then_inc(s_qs, 1)

            def lengths(g, s):
                h, i = head(g, s), s % G
                pool.wait_ge(s_ve2, h + 1)
                power(rstd2[:, i:i + 1], ve2[:, i:i + 1], s_rs2)
                pool.wait_ge(s_rs2, h + 1)
                shift(shift2[:, i:i + 1], nmean2[:, i:i + 1], rstd2[:, i:i + 1], s_sh2)
                pool.wait_ge(s_nn, h + 1)
                j = s // HEADS
                if not duo_before(g, j, 2):
                    pool.wait_ge(s_rt, ROUTE * (duo_no(g, j) - 2) + 2)
                power(rlen[:, i:i + 1], nn2[:, i:i + 1], s_rl)

            def part_sums(g, s):
                h = head(g, s)
                pool.wait_ge(s_wt, NB * (h + 1))
                if not before(g, s, 1):
                    pool.wait_ge(s_att, h)
                nc.gpsimd.tensor_tensor(att[:], w[:, :, CH:2 * CH], w[:, :, 2 * CH:D4], ALU.add).then_inc(s_d23, 1)

            nc.gpsimd.memset(minus_half[:], -0.5).then_inc(s_half, 1)
            nc.gpsimd.memset(half[:], 0.5).then_inc(s_half, 1)
            pool.wait_ge(s_half, 2)
            prep(0, 0)
            q_sums(0, 0)

            def group(g):
                for s in range(G):
                    if exists(g, s + 1):
                        prep(g, s + 1)
                    for k in split_beside[head(g, s - 1)] if before(g, s, len(split_beside) + 1) and head(g, s) else ():
                        pool.wait_ge(s_high, k + 1)
                        high, low, whole = weights[k]
                        nc.gpsimd.tensor_tensor(low, whole, high.bitcast(F32), ALU.subtract).then_inc(s_low, 1)
                    if exists(g, s - 1):
                        lengths(g, s - 1)
                    if exists(g, s + 1):
                        q_sums(g, s + 1)
                    if exists(g, s):
                        part_sums(g, s)

            run(pool, group)

        @block.scalar
        def _(act):
            def q_out(g, s):
                h = head(g, s)
                act.wait_ge(s_qT, h + 1)
                if not before(g, s, 2):
                    act.wait_ge(s_wt, NB * (h - 1))
                src = t_ps[:].rearrange("p (n c) -> p n c", n=NREC)
                nc.scalar.copy(qs[:, s % 2, :, D0:D0 + CH], src).then_inc(s_qev, 1)
                nc.scalar.copy(qs[:, s % 2, :, REC:QREC], src[:, :, 0:3 * BH]).then_inc(s_qev, 1)

            def moments(row, h, k, total, nmean, dev, steps, done):
                nc.scalar.activation(junk[:], row, ACT.Copy, accum_out=total[:, k:k + 1]).then_inc(steps, 1)
                act.wait_ge(steps, 2 * h + 1)
                nc.scalar.mul(nmean[:, k:k + 1], total[:, k:k + 1], -1.0 / L).then_inc(steps, 1)
                act.wait_ge(steps, 2 * h + 2)
                nc.scalar.activation(junk[:], row, ACT.Square, bias=nmean[:, k:k + 1], accum_out=dev[:, k:k + 1])\
                    .then_inc(done, 1)

            def moments1(g, s):
                h, k = head(g, s), s % 2
                act.wait_ge(s_x[s % G], 16 * loads(g, s, G))
                if not before(g, s, 2):
                    act.wait_ge(s_qn, h - 1)
                if not before(g, s, 3):
                    act.wait_ge(s_dev2, h - 2)
                elif h:
                    act.wait_ge(s_dev1, h)
                moments(x_in[:, s % G, :], h, k, total1, nmean1, dev1, s_mo1, s_dev1)

            def moments2(g, s):
                h, i = head(g, s), s % G
                act.wait_ge(s_x2, h + 1)
                act.wait_ge(s_dev1, min(h + 3, H) if isinstance(g, int) else h + 3)
                moments(x_in[:, i, :], h, i, total2, nmean2, dev2, s_mo2, s_dev2)

            def split_pairs(g, s):
                h, k = head(g, s), s % 2
                act.wait_ge(s_prod, h + 1)
                nc.scalar.copy(pair[0][:, k], prod[:, k]).then_inc(s_ph, 1)

            def norm(out, row, rstd, shift, done):
                nc.scalar.activation(out, row, ACT.Identity, bias=shift, scale=rstd).then_inc(done, 1)

            def norm_q(g, s):
                h, k = head(g, s), s % 2
                act.wait_ge(s_sh1, h + 1)
                if not before(g, s, 1):
                    act.wait_ge(s_qT, h)
                norm(qn[:], x_in[:, s % G, :], rstd1[:, k:k + 1], shift1[:, k:k + 1], s_qn)

            def norm_x(g, j, i):
                k, n = tile(j, i), duo_no(g, j) * HEADS + i
                act.wait_ge(s_sh2, n + 1)
                if i == 0:
                    act.wait_ge(s_dev2, n + 2)
                if not (duo_before(g, j, 1) and i == 0):
                    act.wait_ge(s_xT, n)
                norm(xn[:], x_in[:, k, :], rstd2[:, k:k + 1], shift2[:, k:k + 1], s_xn)

            def keep(g, j, i):
                k, n = tile(j, i), head(g, HEADS * j + i)
                act.wait_ge(s_x2, n + 1)
                if not duo_before(g, j, 2):
                    act.wait_ge(s_out[k], 16 * (g + j // 2))
                nc.scalar.copy(res[:, k, :], x_in[:, k, :]).then_inc(s_res, 1)

            def xn_out(g, j, i):
                act.wait_ge(s_xT, duo_no(g, j) * HEADS + i + 1)
                if not duo_before(g, j, 2):
                    act.wait_ge(s_e, USES * (duo_no(g, j) - 2) + E)
                nc.scalar.copy(xn_t[0][:, j % 2, :, i * P:(i + 1) * P], m_ps[:].rearrange("p (c t) -> p c t", c=NB))\
                    .then_inc(s_xev, 1)

            def exponentials(g, j):
                act.wait_ge(s_rt, ROUTE * duo_no(g, j) + 5)
                nc.scalar.activation(ex[:], lg[:, 1], ACT.Exp).then_inc(s_ex, 1)

            def combine_out(g, j):
                act.wait_ge(s_cT, duo_no(g, j) + 1)
                if not duo_before(g, j, 1):
                    act.wait_ge(s_cD, 16 * duo_no(g, j))
                nc.scalar.copy(comb_t[:], m_ps[0:E, 0:ROWS]).then_inc(s_cS, 1)

            def hidden_high(g, j, e):
                act.wait_ge(s_eu, USES * duo_no(g, j) + e + 2)
                nc.scalar.copy(hs[0][:, e:e + 2, :], hw[:, e:e + 2, :]).then_inc(s_hh, 1)

            def front(step, g, s, *n):
                if duo_exists(g, s // HEADS - 1):
                    step(g, s // HEADS - 1, *n)

            def back(step, g, s, *n):
                if duo_exists(g, s // HEADS - 2):
                    step(g, s // HEADS - 2, *n)

            def split_weights(g, s):
                for k in split_beside[head(g, s)] if before(g, s, len(split_beside)) else ():
                    act.wait_ge(s_load[k], 16)
                    nc.scalar.copy(weights[k][0], weights[k][2]).then_inc(s_high, 1)

            def even_head(g, s):
                if exists(g, s + 1):
                    moments1(g, s + 1)
                front(keep, g, s, 0)
                if exists(g, s + 1):
                    norm_q(g, s + 1)
                back(hidden_high, g, s, 0)
                if exists(g, s - 1):
                    moments2(g, s - 1)
                front(norm_x, g, s, 0)
                if exists(g, s + 1):
                    q_out(g, s + 1)
                back(hidden_high, g, s, 2)
                if exists(g, s + 1):
                    split_pairs(g, s + 1)
                front(xn_out, g, s, 0)
                front(norm_x, g, s, 1)
                back(hidden_high, g, s, 4)
                front(xn_out, g, s, 1)
                split_weights(g, s)

            def odd_head(g, s):
                if exists(g, s + 1):
                    moments1(g, s + 1)
                back(hidden_high, g, s, 6)
                if exists(g, s + 1):
                    norm_q(g, s + 1)
                if exists(g, s - 1):
                    moments2(g, s - 1)
                front(keep, g, s, 1)
                front(exponentials, g, s)
                if exists(g, s + 1):
                    split_pairs(g, s + 1)
                    q_out(g, s + 1)
                front(combine_out, g, s)
                split_weights(g, s)

            def group(g):
                for s in range(G):
                    (odd_head if s % HEADS else even_head)(g, s)

            moments1(0, 0)
            norm_q(0, 0)
            split_pairs(0, 0)
            q_out(0, 0)
            run(act, group)

        @block.tensor
        def _(pe):
            def transpose_blocks(out, block_of, done):
                for n in range(NB):
                    turned = pe.matmul(out[:, n * P:(n + 1) * P], block_of(n), ident, start=(n == 0),
                                       stop=(n == NB - 1), is_transpose=True, skip_group_check=True)
                turned.then_inc(done, 1)

            def turn_q(g, s):
                h = head(g, s)
                pe.wait_ge(s_qn, h + 1)
                if not before(g, s, 2):
                    pe.wait_ge(s_x2, h - 1)
                transpose_blocks(t_ps, lambda n: qn[:, n * P:(n + 1) * P], s_qT)

            def convolve(g, s, r):
                h = head(g, s)
                if r == 0:
                    pe.wait_ge(s_t[s % 2], 32 * loads(g, s, 2))
                    pe.wait_ge(s_pair, h + 1)
                if not (before(g, s, 1) and r < 2):
                    pe.wait_ge(s_wt, NB * h + r - 1)
                for f in range(HALF):
                    for n in range(r + 1):
                        for a, b in PARTS:
                            product = pe.matmul(y_ps[r % 2][f][:, 0:REC], toep[a][:, s % 2, (r - n) * P:(r - n + 1) * P],
                                                pair[b][:, s % 2, n * HALF + f, :], start=(n == 0 and (a, b) == PARTS[0]),
                                                stop=(n == r and (a, b) == PARTS[-1]))
                product.then_inc(s_y, 1)

            def turn_attention(g, s):
                h = head(g, s)
                pe.wait_ge(s_sum, SUMS * (h + 1))
                pe.wait_ge(s_qev, 2 * min(h + 2, H) if isinstance(g, int) else 2 * (h + 2))
                transpose_blocks(t_ps, lambda n: att[:, n * HALF:(n + 1) * HALF, :], s_att)

            def turn_x(g, j, i):
                n = duo_no(g, j) * HEADS + i
                pe.wait_ge(s_xn, n + 1)
                if i > 0:
                    pe.wait_ge(s_xlo, n)
                elif not duo_before(g, j, 1):
                    pe.wait_ge(s_cS, duo_no(g, j))
                transpose_blocks(m_ps, lambda b: xn[:, b * P:(b + 1) * P], s_xT)

            def logits(g, j):
                pe.wait_ge(s_xlo, HEADS * (duo_no(g, j) + 1))
                if duo_before(g, j, 1):
                    pe.wait_ge(s_low, 1)
                for i in range(HEADS):
                    for n in range(NB):
                        for a in range(2):
                            product = pe.matmul(m_ps[:, 2 * i * E:(2 * i + 2 - a) * E], xn_t[a][:, j % 2, n, i * P:(i + 1) * P],
                                                wr[:, n, 0:2 - a, :], start=(i == 0 and n == 0 and a == 0),
                                                stop=(i == HEADS - 1 and n == NB - 1 and a == 1), skip_group_check=True)
                product.then_inc(s_lg, 1)

            def turn_combine(u):
                pe.wait_ge(s_rt, ROUTE * (u + 1))
                for i in range(HEADS):
                    turned = pe.matmul(m_ps[0:E, i * P:(i + 1) * P], comb[:, i, :], ident, start=(i == 0),
                                       stop=(i == HEADS - 1), is_transpose=True, skip_group_check=True)
                turned.then_inc(s_cT, 1)

            def expert_bank(g, j, use):
                if use >= 2 or not duo_before(g, j, 1):
                    pe.wait_ge(s_eu, USES * duo_no(g, j) + use - 1)

            def hidden(g, j, e):
                if e == 0 and duo_before(g, j, 1):
                    pe.wait_ge(s_low, 1 + NB)
                expert_bank(g, j, e)
                for c in range(NB):
                    for a, b in PARTS:
                        product = pe.matmul(e_ps[e % 2][:, 0:ROWS], wa[a][:, c, e, :], xn_t[b][:, j % 2, c, :],
                                            start=(c == 0 and (a, b) == PARTS[0]), stop=(c == NB - 1 and (a, b) == PARTS[-1]))
                product.then_inc(s_e, 1)

            def outputs(g, j, i, part):
                if part == 0:
                    expert_bank(g, j, E + i)
                if i == 0 and duo_before(g, j, 1):
                    pe.wait_ge(s_low, len(weights))
                if i == 0:
                    pe.wait_ge(s_hl, E // 2 * duo_no(g, j) + E // 4 * (part + 1))
                experts = range(part * E // 2, (part + 1) * E // 2)
                for e in experts:
                    for a, b in PARTS:
                        product = pe.matmul(e_ps[i][:], hs[a][:, e, i * P:(i + 1) * P], wb[b][:, e, :],
                                            start=(e == 0 and (a, b) == PARTS[0]), stop=(e == E - 1 and (a, b) == PARTS[-1]))
                if part == 1:
                    product.then_inc(s_e, 1)

            def experts(g, s, r):
                for what, j, n in expert_steps(g, s, r):
                    if what == "T":
                        turn_x(g, j, n)
                    if what == "L":
                        logits(g, j)
                    if what == "R":
                        turn_combine(duo_no(g, j))
                    if what == "S":
                        hidden(g, j, n)
                    if what == "O":
                        outputs(g, j, *n)

            def group(g):
                for s in range(G):
                    for r in range(NB):
                        if exists(g, s):
                            convolve(g, s, r)
                        if r == 1 and exists(g, s - 1):
                            turn_attention(g, s - 1)
                        if r == 2 and exists(g, s + 1):
                            turn_q(g, s + 1)
                        experts(g, s, r)

            pe.wait_ge(s_const, 16)
            turn_q(0, 0)
            run(pe, group)

        @block.vector
        def _(dve):
            def var_eps(h, k, dev, ve, s_dev, s_ve):
                dve.wait_ge(s_dev, h + 1)
                nc.vector.tensor_scalar(ve[:, k:k + 1], dev[:, k:k + 1], 1.0 / L, EPS, ALU.mult, ALU.add).then_inc(s_ve, 1)

            def products_1(g, s):
                if before(g, s, 2) and s == 1:
                    dve.wait_ge(s_padw, 32)
                dve.wait_ge(s_c[s % 2], 16 * loads(g, s, 2))
                product(s, 1)
                product(s, 2)

            def product(s, d):
                c = c_in[:, s % 2]
                nc.vector.tensor_tensor(prod[:, s % 2, :, (d - 1) * CH:d * CH], c[:, :, 0:CH],
                                        c[:, :, d * BH:d * BH + CH], ALU.mult)

            def products_2(g, s):
                c, p = c_in[:, s % 2], prod[:, s % 2]
                product(s, 3)
                nc.vector.tensor_tensor(p[:, :, D4:D0], c[:, :, 0:32], c[:, :, 32:64], ALU.mult)

            def products_3(g, s):
                h = head(g, s)
                c, p = c_in[:, s % 2], prod[:, s % 2]
                dve.wait_ge(s_cd, h + 1)
                nc.vector.scalar_tensor_tensor(p[:, :, D0:REC], p[:, :, D0:REC], 2.0, c[:, :, 0:CH], ALU.mult, ALU.mult)\
                    .then_inc(s_prod, 1)

            def split_pairs(g, s):
                h, k = head(g, s), s % 2
                dve.wait_ge(s_ph, h + 1)
                nc.vector.tensor_tensor(pair[1][:, k], prod[:, k], pair[0][:, k].bitcast(F32), ALU.subtract)\
                    .then_inc(s_pair, 1)

            def weigh(g, s, r):
                h = head(g, s)
                dve.wait_ge(s_y, NB * h + r + 1)
                if r == 0:
                    dve.wait_ge(s_qs, NB * (h + 1))
                    if not before(g, s, 1):
                        dve.wait_ge(s_sum, SUMS * h)
                for f in range(HALF):
                    n = r * HALF + f
                    weighted = nc.vector.tensor_tensor(w[:, n, :], y_ps[r % 2][f][:, 0:REC], qs[:, s % 2, n, 0:REC], ALU.mult)
                weighted.then_inc(s_wt, 1)

            def sum_pairs(g, s, part):
                h = head(g, s)
                a = w[:, :, D0:REC]
                a2 = a.rearrange("p n (t c) -> p n t c", t=2)
                first = SUMS * h

                def add(out, in0, in1, after):
                    if after:
                        dve.wait_ge(s_sum, first + after)
                    nc.vector.tensor_tensor(out, in0, in1, ALU.add).then_inc(s_sum, 1)

                if part == 0:
                    dve.wait_ge(s_wt, NB * (h + 1))
                    add(a, a, w[:, :, 0:CH], 0)
                    add(a2, a2, w[:, :, D4:D0].unsqueeze(2).to_broadcast([P, NREC, 2, CH // 2]), 1)
                if part == 1:
                    dve.wait_ge(s_d23, h + 1)
                    add(a, a, att[:], 2)
                for d in {0: (), 1: (1,), 2: (2, 3)}[part]:
                    k, lo, after = d * BH, (d - 1) * CH, 2 * d + 1
                    out = att[:] if d == 3 else a
                    add(out[:, :, k:CH], a[:, :, k:CH], w[:, :, lo:lo + CH - k], after)
                    add(out[:, :, 0:k], a[:, :, 0:k], w[:, :, lo + CH - k:lo + CH], after)

            def residual(g, s):
                h, i = head(g, s), s % G
                dve.wait_ge(s_att, h + 1)
                nc.vector.tensor_tensor(x_in[:, i, :], t_ps[:], x_in[:, i, :], ALU.add).then_inc(s_x2, 1)

            def lengths(g, s):
                h, i = head(g, s), s % G
                dve.wait_ge(s_rs2, h + 1)
                nc.vector.scalar_tensor_tensor(nn[:, i:i + 1], rstd2[:, i:i + 1], rstd2[:, i:i + 1], dev2[:, i:i + 1],
                                               ALU.mult, ALU.mult).then_inc(s_nn0, 1)
                dve.wait_ge(s_nn0, h + 1)
                nc.vector.tensor_scalar(nn2[:, i:i + 1], nn[:, i:i + 1], 1e-24, None, ALU.max).then_inc(s_nn, 1)

            def xn_low(g, j, i):
                dve.wait_ge(s_xev, HEADS * duo_no(g, j) + i + 1)
                cols = slice(i * P, (i + 1) * P)
                nc.vector.tensor_tensor(xn_t[1][:, j % 2, :, cols], m_ps[:].rearrange("p (c t) -> p c t", c=NB),
                                        xn_t[0][:, j % 2, :, cols].bitcast(F32), ALU.subtract).then_inc(s_xlo, 1)

            def scale_logits(g, j):
                u, k = duo_no(g, j), tile(j, 0)
                dve.wait_ge(s_lg, u + 1)
                dve.wait_ge(s_rl, HEADS * (u + 1))
                for part in range(2):
                    nc.vector.tensor_tensor(lg[:, 4 + part], m_ps[:, 0:2 * HEADS * E].rearrange("p (i k e) -> p i k e", i=HEADS, e=E)[:, :, part],
                                            rlen[:, k:k + HEADS].unsqueeze(2).to_broadcast([P, HEADS, E]), ALU.mult)\
                        .then_inc(s_rt, 1)

            def route(g, j):
                scale_logits(g, j)
                u = duo_no(g, j)
                first = ROUTE * u
                done = [2]
                wide = lambda a: a.unsqueeze(2).to_broadcast([P, HEADS, E])
                lower = preference.unsqueeze(1).to_broadcast([P, HEADS, E])

                def step(ins):
                    done[0] += 1
                    ins.then_inc(s_rt, 1)
                    dve.wait_ge(s_rt, first + done[0])

                dve.wait_ge(s_rt, first + 2)
                step(nc.vector.tensor_tensor(lg[:, 0], lg[:, 4], lg[:, 5], ALU.add))
                step(nc.vector.tensor_reduce(red[:, 0], lg[:, 0], AX_X, ALU.max))
                step(nc.vector.tensor_tensor(lg[:, 1], lg[:, 0], wide(red[:, 0]), ALU.subtract))
                step(nc.vector.scalar_tensor_tensor(lg[:, 2], lg[:, 1], 0.0, lower, ALU.is_ge, ALU.mult))
                step(nc.vector.tensor_reduce(red[:, 1], lg[:, 2], AX_X, ALU.max))
                step(nc.vector.tensor_tensor(lg[:, 3], lg[:, 2], wide(red[:, 1]), ALU.is_equal))
                step(nc.vector.scalar_tensor_tensor(lg[:, 4], lg[:, 3], -HUGE, lg[:, 1], ALU.mult, ALU.add))
                step(nc.vector.tensor_reduce(red[:, 2], lg[:, 4], AX_X, ALU.max))
                step(nc.vector.tensor_tensor(lg[:, 5], lg[:, 4], wide(red[:, 2]), ALU.is_equal))
                step(nc.vector.tensor_tensor(lg[:, 2], lg[:, 5], lower, ALU.mult))
                step(nc.vector.tensor_reduce(red[:, 3], lg[:, 2], AX_X, ALU.max))
                step(nc.vector.tensor_tensor(lg[:, 4], lg[:, 2], wide(red[:, 3]), ALU.is_equal))
                step(nc.vector.tensor_tensor(lg[:, 0], lg[:, 3], lg[:, 4], ALU.add))
                dve.wait_ge(s_ex, u + 1)
                step(nc.vector.tensor_tensor(lg[:, 5], ex[:], lg[:, 0], ALU.mult))
                step(nc.vector.reduce_sum(red[:, 4], lg[:, 5], AX_X))
                step(nc.vector.reciprocal(red[:, 5], red[:, 4]))
                step(nc.vector.tensor_tensor(comb[:], lg[:, 5], wide(red[:, 5]), ALU.mult))

            def weigh_hidden(g, j, e):
                u = duo_no(g, j)
                dve.wait_ge(s_e, USES * u + e + 1)
                dve.wait_ge(s_cw[e // (E // 2)], 16 * (u + 1))
                nc.vector.tensor_tensor(hw[:, e, :], e_ps[e % 2][:, 0:ROWS], cw[:, e, :], ALU.mult)\
                    .then_inc(s_eu, 1)

            def finish(g, j, i):
                k = tile(j, i)
                dve.wait_ge(s_e, USES * duo_no(g, j) + E + i + 1)
                dve.wait_ge(s_res, head(g, HEADS * j + i) + 1)
                nc.vector.tensor_tensor(res[:, k, :], e_ps[i][:], res[:, k, :], ALU.add).then_inc(s_eu, 1)

            nc.vector.memset(kp[:, 0:P], 0.0)
            dve.wait_ge(s_taps, 32)
            nc.vector.tensor_tensor(kp[:, P:P + 1], kp[:, P:P + 1], skips[:], ALU.add).then_inc(s_padd, 1)
            dve.wait_ge(s_padd, 1)
            nc.vector.tensor_copy(kpp[0], kp).then_inc(s_padd, 1)
            dve.wait_ge(s_padd, 2)
            nc.vector.tensor_tensor(kpp[1], kp, kpp[0].bitcast(F32), ALU.subtract).then_inc(s_padd, 1)
            var_eps(0, 0, dev1, ve1, s_dev1, s_ve1)
            products_1(0, 0)
            products_2(0, 0)
            products_3(0, 0)
            split_pairs(0, 0)

            def hidden_low(g, j, e):
                dve.wait_ge(s_hh, E // 2 * duo_no(g, j) + e // 2 + 1)
                nc.vector.tensor_tensor(hs[1][:, e:e + 2, :], hw[:, e:e + 2, :],
                                        hs[0][:, e:e + 2, :].bitcast(F32), ALU.subtract).then_inc(s_hl, 1)

            def front(step, g, s, *n):
                if duo_exists(g, s // HEADS - 1):
                    step(g, s // HEADS - 1, *n)

            def back(step, g, s, *n):
                if duo_exists(g, s // HEADS - 2):
                    step(g, s // HEADS - 2, *n)

            def even_head(g, s):
                this, following, preceding = exists(g, s), exists(g, s + 1), exists(g, s - 1)
                if following:
                    var_eps(head(g, s + 1), (s + 1) % 2, dev1, ve1, s_dev1, s_ve1)
                if preceding:
                    sum_pairs(g, s - 1, 2)
                if this:
                    weigh(g, s, 0)
                back(weigh_hidden, g, s, 0)
                back(weigh_hidden, g, s, 1)
                if following:
                    products_1(g, s + 1)
                if preceding:
                    residual(g, s - 1)
                back(hidden_low, g, s, 0)
                back(weigh_hidden, g, s, 2)
                if this:
                    weigh(g, s, 1)
                back(weigh_hidden, g, s, 3)
                if following:
                    products_2(g, s + 1)
                if preceding:
                    var_eps(head(g, s - 1), (s - 1) % G, dev2, ve2, s_dev2, s_ve2)
                if following:
                    products_3(g, s + 1)
                if preceding:
                    lengths(g, s - 1)
                if this:
                    weigh(g, s, 2)
                back(hidden_low, g, s, 2)
                back(weigh_hidden, g, s, 4)
                if following:
                    split_pairs(g, s + 1)
                back(weigh_hidden, g, s, 5)
                front(xn_low, g, s, 0)
                back(hidden_low, g, s, 4)
                if this:
                    weigh(g, s, 3)
                back(weigh_hidden, g, s, 6)
                if this:
                    sum_pairs(g, s, 0)
                back(weigh_hidden, g, s, 7)
                if this:
                    sum_pairs(g, s, 1)
                front(xn_low, g, s, 1)

            def odd_head(g, s):
                this, following, preceding = exists(g, s), exists(g, s + 1), exists(g, s - 1)
                if following:
                    var_eps(head(g, s + 1), (s + 1) % 2, dev1, ve1, s_dev1, s_ve1)
                if preceding:
                    sum_pairs(g, s - 1, 2)
                back(hidden_low, g, s, 6)
                if this:
                    weigh(g, s, 0)
                if following:
                    products_1(g, s + 1)
                if preceding:
                    residual(g, s - 1)
                if this:
                    weigh(g, s, 1)
                if following:
                    products_2(g, s + 1)
                if preceding:
                    var_eps(head(g, s - 1), (s - 1) % G, dev2, ve2, s_dev2, s_ve2)
                if following:
                    products_3(g, s + 1)
                if preceding:
                    lengths(g, s - 1)
                front(route, g, s)
                if this:
                    weigh(g, s, 2)
                back(finish, g, s, 0)
                if following:
                    split_pairs(g, s + 1)
                if this:
                    weigh(g, s, 3)
                    sum_pairs(g, s, 0)
                back(finish, g, s, 1)
                if this:
                    sum_pairs(g, s, 1)

            def group(g):
                for s in range(G):
                    (odd_head if s % HEADS else even_head)(g, s)

            run(dve, group)


def kernel(x, ctx_2048, L0_xattn_ssm_kernel, L0_xattn_D, L0_ffn_router_w, L0_ffn_Wa, L0_ffn_Wb):
    import numpy as np
    import concourse.bacc as bacc
    from concourse.bass_utils import run_bass_kernel_spmd

    x_t = np.asarray(x).reshape(HALF, BH, H, HD, L).transpose(2, 0, 3, 1, 4).reshape(H, P, L)
    c = np.asarray(ctx_2048).reshape(HALF, BH, H, HD, NB, P)[..., ::-1].transpose(2, 5, 4, 0, 3, 1)
    c_t = np.concatenate([c, c[:, :, :, :, 0:3]], axis=4).reshape(H, P, NREC * CREC)
    consts = np.concatenate([np.eye(P, dtype=np.float32),
                             np.tile(np.arange(E, 0, -1, dtype=np.float32), (P, 1))], axis=1)
    ins = {"x_t": x_t, "c_t": c_t, "taps": np.asarray(L0_xattn_ssm_kernel), "skip": np.asarray(L0_xattn_D).reshape(H, 1),
           "w_r": np.asarray(L0_ffn_router_w), "w_a": np.asarray(L0_ffn_Wa), "w_b": np.asarray(L0_ffn_Wb),
           "consts": consts}
    nc = bacc.Bacc("TRN2", target_bir_lowering=False, num_devices=1)
    arrays, args = {}, []
    for name, a in ins.items():
        a = np.ascontiguousarray(a)
        arrays[f"in_{name}_dram"] = a
        args.append(nc.dram_tensor(f"in_{name}_dram", a.shape, mybir.dt.from_np(a.dtype), kind="ExternalInput").ap())
    args.append(nc.dram_tensor("out_dram", [H, P, L], F32, kind="ExternalOutput").ap())
    build(nc, *args)
    r = run_bass_kernel_spmd(nc, [arrays], core_ids=[0])
    got = np.asarray(r.results[0]["out_dram"]).reshape(H, HALF, HD, BH, L)
    return np.ascontiguousarray(got.transpose(1, 3, 0, 2, 4).reshape(B, H * HD, L))
```
